# Optimizing a Trainium2 kernel written in Bass

```python
import numpy as np
import jax
import jax.numpy as jnp

def _softmax(x, axis=-1):
    return jax.nn.softmax(x, axis=axis)

def _gelu(x):
    return jax.nn.gelu(x, approximate=True)

def _silu(x):
    return jax.nn.silu(x)

def _sigmoid(x):
    return jax.nn.sigmoid(x)

def _layernorm(x, axis=-1, eps=1e-05):
    m = jnp.mean(x, axis=axis, keepdims=True)
    v = jnp.var(x, axis=axis, keepdims=True)
    return (x - m) / jnp.sqrt(v + eps)

def _scatter_add(tgt, idx, src, axis=0):
    return tgt.at[idx].add(src)

def _segment_sum(src, seg, n):
    return jax.ops.segment_sum(src, seg, n)
kernel_name = 'mk_macaron_d1_jaxref_r8_ae8249'

def setup_inputs(seed: int=0):
    np.random.seed(seed)
    _w = jnp.asarray

    def _L0_attn_setup():
        import jax, jax.numpy as jnp
        import numpy as np
        B, L, H, U = (4, 512, 128, 128)
        key = jax.random.key(seed)
        k0, k1, k2, k3 = jax.random.split(key, 4)
        inputs = jax.random.normal(k0, (B, L, H), dtype=jnp.float32)
        W_rkv = jax.random.normal(k1, (H, 3 * U), dtype=jnp.float32) / np.sqrt(H)
        b_rkv = jnp.zeros((3 * U,), dtype=jnp.float32)
        W_o = jax.random.normal(k2, (U, H), dtype=jnp.float32) / np.sqrt(U)
        b_o = jnp.zeros((H,), dtype=jnp.float32)
        r_min, r_max = (0.9, 0.999)
        u = jax.random.uniform(k3, (U,), dtype=jnp.float32)
        nu_log = jnp.log(-0.5 * jnp.log(u * (r_max ** 2 - r_min ** 2) + r_min ** 2))
        gamma_log = jnp.zeros((U,), dtype=jnp.float32)
        return {'inputs': inputs, 'W_rkv': W_rkv, 'b_rkv': b_rkv, 'W_o': W_o, 'b_o': b_o, 'nu_log': nu_log, 'gamma_log': gamma_log}
    _L0_attn_in = _L0_attn_setup()

    def _L0_ffn_setup():
        import jax, jax.numpy as jnp
        import numpy as np
        EPS = 1e-06
        N_EXPERTS = 8

        def _rms_norm(x, scale, eps=EPS):
            mean_sq = jnp.mean(x.astype(jnp.float32) ** 2, axis=-1, keepdims=True)
            s = scale.astype(jnp.float32) * jax.lax.rsqrt(mean_sq + eps)
            return x * s.astype(x.dtype)

        def _dist2(x, y):
            nx = jnp.sum(x ** 2, axis=-1)[..., :, None]
            ny = jnp.sum(y ** 2, axis=-1)[..., None, :]
            return nx + ny - 2.0 * (x @ y.T)
        key = jax.random.key(seed)
        ks = jax.random.split(key, 5)
        dim, hidden, E = (128, 256, N_EXPERTS)
        x = jax.random.normal(ks[0], (4, 256, dim), dtype=jnp.float32)
        scale = jnp.ones((dim,), dtype=jnp.float32)
        centroids = jax.random.normal(ks[1], (E, dim), dtype=jnp.float32)
        up_w = jax.random.normal(ks[2], (E, dim, hidden * 2), dtype=jnp.float32) * dim ** (-0.5)
        down_w = jax.random.normal(ks[3], (E, hidden, dim), dtype=jnp.float32) * hidden ** (-0.5)
        return {'x': x, 'scale': scale, 'centroids': centroids, 'up_w': up_w, 'down_w': down_w}
    _L0_ffn_in = _L0_ffn_setup()
    _d = {'L0_attn_inputs': _L0_attn_in['inputs'], 'L0_attn_W_rkv': _L0_attn_in['W_rkv'], 'L0_attn_b_rkv': _L0_attn_in['b_rkv'], 'L0_attn_W_o': _L0_attn_in['W_o'], 'L0_attn_b_o': _L0_attn_in['b_o'], 'L0_attn_nu_log': _L0_attn_in['nu_log'], 'L0_attn_gamma_log': _L0_attn_in['gamma_log'], 'L0_ffn_scale': _L0_ffn_in['scale'], 'L0_ffn_centroids': _L0_ffn_in['centroids'], 'L0_ffn_up_w': _L0_ffn_in['up_w'], 'L0_ffn_down_w': _L0_ffn_in['down_w']}
    _x0 = _d['L0_attn_inputs']
    _d['L0_attn_inputs'] = jax.random.normal(jax.random.fold_in(jax.random.key(seed), 1), (8, 512, 128), dtype=_x0.dtype)
    del _x0
    return _d

def reference(L0_attn_inputs, L0_attn_W_rkv, L0_attn_b_rkv, L0_attn_W_o, L0_attn_b_o, L0_attn_nu_log, L0_attn_gamma_log, L0_ffn_scale, L0_ffn_centroids, L0_ffn_up_w, L0_ffn_down_w):

    def _L0_attn_ref(inputs, W_rkv, b_rkv, W_o, b_o, nu_log, gamma_log):
        import jax, jax.numpy as jnp
        import numpy as np
        B, L, H, U = (4, 512, 128, 128)
        rkv = jnp.einsum('blh,hu->blu', inputs, W_rkv) + b_rkv
        r, k, v = jnp.split(rkv, 3, axis=-1)
        r = jax.nn.sigmoid(r)
        k = jnp.exp(k)
        kv = k * v
        u = jnp.concatenate([kv, k], axis=-1)
        nu = jnp.exp(jnp.concatenate([nu_log, nu_log]))
        gamma = jnp.exp(nu_log + gamma_log) - 1.0
        lam = jnp.exp(-nu)
        a = jnp.broadcast_to(lam, u.shape)

        def combine(c1, c2):
            a1, x1 = c1
            a2, x2 = c2
            return (a1 * a2, x1 * a2 + x2)
        _, y = jax.lax.associative_scan(combine, (a, u), axis=1)
        u1, u2 = jnp.split(y, 2, axis=-1)
        x = (u1 + gamma * kv) / (u2 + gamma * k + 1e-06) * r
        return jnp.einsum('blu,uh->blh', x, W_o) + b_o

    def _L0_ffn_ref(x, scale, centroids, up_w, down_w):
        import jax, jax.numpy as jnp
        import numpy as np
        EPS = 1e-06
        N_EXPERTS = 8

        def _rms_norm(x, scale, eps=EPS):
            mean_sq = jnp.mean(x.astype(jnp.float32) ** 2, axis=-1, keepdims=True)
            s = scale.astype(jnp.float32) * jax.lax.rsqrt(mean_sq + eps)
            return x * s.astype(x.dtype)

        def _dist2(x, y):
            nx = jnp.sum(x ** 2, axis=-1)[..., :, None]
            ny = jnp.sum(y ** 2, axis=-1)[..., None, :]
            return nx + ny - 2.0 * (x @ y.T)
        skip = x
        xn = _rms_norm(x, scale)
        ids = jnp.argmin(_dist2(xn, centroids), axis=-1)
        out = jnp.zeros_like(x)
        for e in range(N_EXPERTS):
            h = jnp.einsum('bsd,dh->bsh', xn, up_w[e])
            a, g = jnp.split(h, 2, axis=-1)
            y = jnp.einsum('bsh,hd->bsd', a * jax.nn.silu(g), down_w[e])
            out = jnp.where((ids == e)[..., None], y, out)
        return out + skip
    x = L0_attn_inputs
    x = x + 0.5 * _L0_ffn_ref(_layernorm(x, axis=-1), L0_ffn_scale, L0_ffn_centroids, L0_ffn_up_w, L0_ffn_down_w)
    x = x + _L0_attn_ref(_layernorm(x, axis=-1), L0_attn_W_rkv, L0_attn_b_rkv, L0_attn_W_o, L0_attn_b_o, L0_attn_nu_log, L0_attn_gamma_log)
    x = x + 0.5 * _L0_ffn_ref(_layernorm(x, axis=-1), L0_ffn_scale, L0_ffn_centroids, L0_ffn_up_w, L0_ffn_down_w)
    return x

_drawn_inputs = setup_inputs


def setup_inputs(seed=0):
    import zlib

    import numpy as np

    out = dict(_drawn_inputs(seed))
    spreads = {'L0_attn_b_rkv': (0.0, 0.1),
     'L0_attn_b_o': (0.0, 0.1),
     'L0_attn_gamma_log': (0.0, 2.0),
     'L0_ffn_scale': (1.0, 0.2)}
    factors = {}
    for name, (base, spread) in spreads.items():
        noise = np.random.default_rng([zlib.crc32(name.encode()), seed]).standard_normal(out[name].shape)
        drawn = base * np.exp(spread * noise) if base else spread * noise
        out[name] = jnp.asarray(drawn.astype(out[name].dtype))
    for name, factor in factors.items():
        out[name] = (out[name] * factor).astype(out[name].dtype)
    return out
```

```python
import concourse.bass as bass
import numpy as np
from concourse import mybir
from contextlib import ExitStack

F32 = mybir.dt.float32
F32R = mybir.dt.float32r
BF16 = mybir.dt.bfloat16
I32 = mybir.dt.int32
ALU = mybir.AluOpType
ACT = mybir.ActivationFunctionType
AX = mybir.AxisListType

P = 128
B, L, D = 8, 512, 128
E, HID = 8, 256
TOKENS = B * L
TILES = TOKENS // P
BT = L // P
SLOT_TILES = TILES + E - 1
FFNS = 2
LN_EPS, RMS_EPS, DEN_EPS = 1e-5, 1e-6, 1e-6
RSQRT_SEED = float(0x5F3759DF)

GATHER_BUFS = 6
XT_BUFS = 3
HT_BUFS = 3
OUT_GROUP = 3
OUT_BUFS = 2 * OUT_GROUP
OUT_GROUPS = SLOT_TILES // OUT_GROUP
X_GROUP = 4
XW = D + 1


class Counter:

    def __init__(self, engine, sem):
        self.engine, self.sem, self.n = engine, sem, 0

    def mark(self, instruction):
        instruction.then_inc(self.sem, 1)
        self.n += 1
        return self.n

    def after(self, n):
        self.engine.wait_ge(self.sem, n)


def macaron(nc, x_in, w_rkv, b_rkv, w_o, b_o, nu_log, gamma_log, ffn_scale, centroids, up_w, down_w, out):
    xn_dram = [nc.dram_tensor(f"xn_scratch_{f}", (TOKENS, D), F32, kind="Internal").ap() for f in range(FFNS)]
    y_dram = [nc.dram_tensor(f"y_scratch_{f}", (SLOT_TILES * P, D), F32, kind="Internal").ap() for f in range(FFNS)]

    x_tiles = x_in.rearrange("b (t p) d -> p (b t) d", p=P)
    out_tiles = out.rearrange("b (t p) d -> p (b t) d", p=P)
    xn_tiles = [a.rearrange("(t p) d -> p t d", p=P) for a in xn_dram]
    y_tiles = [a.rearrange("(t p) d -> p t d", p=P) for a in y_dram]

    with ExitStack() as ctx:
        def sb(name, shape, dt=F32):
            return ctx.enter_context(nc.sbuf_tensor(name, shape, dt))

        def pb(name):
            return ctx.enter_context(nc.psum_tensor(name, [P, 512], F32))

        def sem(name):
            return ctx.enter_context(nc.semaphore(name))

        x = sb("x", [P, TILES, D])
        xn = sb("xn", [P, TILES, D])
        y = sb("y", [P, TILES, D])
        up_raw = y[:, :, :].rearrange("p t d -> p (t d)").rearrange("p (e h) -> p e h", e=E)
        down_raw = sb("down_raw", [P, E, 2, D])
        up_hi = sb("up_hi", [P, E * 2 * HID], F32R)
        up_lo = sb("up_lo", [P, E * 2 * HID], F32R)
        down_hi = sb("down_hi", [P, E * 2 * D], F32R)
        down_lo = sb("down_lo", [P, E * 2 * D], F32R)
        wrkv = sb("wrkv", [D, 3 * P])
        wo = sb("wo", [P, D])
        bo_row = sb("bo_row", [1, BT, D])
        cent = sb("cent", [E, D])
        cent_t = sb("cent_t", [D, E])
        cent_sq = sb("cent_sq", [D, E])
        cent_rhs = sb("cent_rhs", [D, E])
        cnorm = sb("cnorm", [P, E])
        cols = sb("cols", [P, 8])
        nu_c, gam_c, scale_c, br_c, bk_c, bv_c = (cols[:, i:i + 1] for i in range(6))
        lam = sb("lam", [P, 1])
        gamma = sb("gamma", [P, 1])
        neg_br = sb("neg_br", [P, 1])
        col_tmp = sb("col_tmp", [P, 2])
        lam_row = sb("lam_row", [P, L])
        ident = sb("ident", [P, P])
        ones_f = sb("ones_f", [P, TILES * E])
        ones_b = sb("ones_b", [P, P], BF16)
        before = sb("before", [P, P], BF16)
        iota_slot = sb("iota_slot", [P, P], BF16)
        iota_tile = sb("iota_tile", [P, SLOT_TILES])
        iota_tok_tile = sb("iota_tok_tile", [P, TILES, SLOT_TILES], BF16)
        iota_part = sb("iota_part", [P, 1])
        rank_code = sb("rank_code", [P, E, TILES])

        stats = sb("stats", [P, TILES, 6])
        mean = sb("mean", [P, TILES])
        diff = sb("diff", [P, TILES])
        var = sb("var", [P, TILES])
        rs_arg = sb("rs_arg", [P, 2, TILES])
        rs_tmp = sb("rs_tmp", [P, 2, TILES])
        rs_int = sb("rs_int", [P, 2, TILES], I32)
        rs_val = sb("rs_val", [P, 2, TILES])
        nbias = sb("nbias", [P, 2, TILES])
        base_s = sb("base_s", [P, TILES])
        xn_t = sb("xn_t", [D, 2, L])

        score = sb("score", [P, E, TILES])
        best = sb("best", [P, TILES])
        code = sb("code", [P, E, TILES])
        onehot = sb("onehot", [P, E, TILES], BF16)
        csum = sb("csum", [P, E, TILES])
        slot = sb("slot", [P, E, TILES])
        starts = sb("starts", [P, E + 1])
        count = sb("count", [P, E])
        tiles_i = sb("tiles_i", [P, E], I32)
        tiles_f = sb("tiles_f", [P, E])
        tile_end = sb("tile_end", [P, E])
        pad = sb("pad", [P, E])
        pos = sb("pos", [P, TILES])
        pos_i = sb("pos_i", [P, TILES], I32)
        hi_i = sb("hi_i", [P, TILES], I32)
        lo_i = sb("lo_i", [P, TILES], I32)
        hi_f = sb("hi_f", [P, TILES])
        lo_f = sb("lo_f", [P, TILES])
        in_tile = sb("in_tile", [P, TILES, SLOT_TILES], BF16)
        tok_id = sb("tok_id", [P, TILES, 2, SLOT_TILES], BF16)
        in_slot = sb("in_slot", [P, TILES, P], BF16)
        src_tok = sb("src_tok", [P, SLOT_TILES], I32)
        past = sb("past", [1, SLOT_TILES, E])
        exp_f = sb("exp_f", [1, SLOT_TILES])
        exp_i = sb("exp_i", [1, SLOT_TILES], I32)

        gathered = sb("gathered", [P, GATHER_BUFS, D])
        xt_hi = sb("xt_hi", [P, XT_BUFS, P], F32R)
        xt_lo = sb("xt_lo", [P, XT_BUFS, P], F32R)
        silu = sb("silu", [P, 2, HID])
        hid = sb("hid", [P, 2, HID])
        ht_hi = sb("ht_hi", [P, HT_BUFS, 2 * P], F32R)
        ht_lo = sb("ht_lo", [P, HT_BUFS, 2 * P], F32R)
        y_out = sb("y_out", [P, OUT_BUFS, D])

        xa = sb("xa", [P, 2, BT, D])
        xa_t = sb("xa_t", [D, 2, L])
        ex_r = sb("ex_r", [P, 2, L])
        ex_k = sb("ex_k", [P, 2, L])
        kv = sb("kv", [P, L])
        u_kv = sb("u_kv", [P, L])
        u_k = sb("u_k", [P, L])
        gate_t = sb("gate_t", [P, 2, L])
        gk = sb("gk", [P, 2, L])

        tr = [pb(f"tr{i}") for i in range(2)]
        up_ps = [pb(f"up_ps{i}") for i in range(2)]
        ht_ps = [pb(f"ht_ps{i}") for i in range(2)]
        y_ps = [pb(f"y_ps{i}") for i in range(2)]
        score_ps, rank_ps = y_ps
        r_ps, k_ps, v_ps, att_ps = up_ps[0], up_ps[1], ht_ps[0], ht_ps[1]

        x_loaded = [sem(f"x_loaded{b}") for b in range(B)]
        cols_loaded = sem("cols_loaded")
        attw_loaded = sem("attw_loaded")
        up_loaded = sem("up_loaded")
        down_loaded = sem("down_loaded")
        const_made = sem("const_made")
        cent_made = sem("cent_made")
        pe_setup = sem("pe_setup")
        act_setup = sem("act_setup")
        dve_setup = sem("dve_setup")
        w_hi = sem("w_hi")
        w_lo = sem("w_lo")
        dve_step = sem("dve_step")
        act_step = sem("act_step")
        scal_ready = sem("scal_ready")
        xn_ready = sem("xn_ready")
        xn_stored = sem("xn_stored")
        xn_transposed = sem("xn_transposed")
        xn_t_ready = sem("xn_t_ready")
        scored = sem("scored")
        base_ready = sem("base_ready")
        onehot_ready = sem("onehot_ready")
        ranks_ready = sem("ranks_ready")
        in_slot_ready = sem("in_slot_ready")
        src_summed = sem("src_summed")
        route_ready = sem("route_ready")
        tile_gathered = [sem(f"tile_gathered{i}") for i in range(GATHER_BUFS)]
        xt_transposed = sem("xt_transposed")
        xt_hi_ready = sem("xt_hi_ready")
        xt_lo_ready = sem("xt_lo_ready")
        up_done = sem("up_done")
        silu_ready = sem("silu_ready")
        hid_ready = sem("hid_ready")
        ht_transposed = sem("ht_transposed")
        ht_hi_ready = sem("ht_hi_ready")
        ht_lo_ready = sem("ht_lo_ready")
        down_done = sem("down_done")
        y_ready = sem("y_ready")
        y_stored = [sem(f"y_stored{i}") for i in range(2)]
        y_gathered = [sem(f"y_gathered{b}") for b in range(B)]
        att_scal = sem("att_scal")
        xa_ready = sem("xa_ready")
        xa_transposed = sem("xa_transposed")
        xa_t_ready = sem("xa_t_ready")
        rkv_done = sem("rkv_done")
        ex_ready = sem("ex_ready")
        gate_ready = sem("gate_ready")
        kv_ready = sem("kv_ready")
        att_done = sem("att_done")
        x2_ready = sem("x2_ready")
        out_ready = sem("out_ready")
        out_stored = sem("out_stored")

        block = ctx.enter_context(nc.Block())

        @block.sync
        def _(sp):
            for src, dst in ((nu_log, nu_c), (gamma_log, gam_c), (ffn_scale, scale_c),
                             (b_rkv[0:P], br_c), (b_rkv[P:2 * P], bk_c), (b_rkv[2 * P:3 * P], bv_c)):
                sp.dma_start(dst, src.rearrange("(p a) -> p a", a=1)).then_inc(cols_loaded, 16)
            sp.dma_start(cent[:, :], centroids).then_inc(cols_loaded, 16)
            for b in range(B):
                sp.dma_start(x[:, BT * b:BT * (b + 1), :], x_tiles[:, BT * b:BT * (b + 1), :]).then_inc(x_loaded[b], 16)
            sp.dma_start(up_raw, up_w.rearrange("e d h -> d e h")).then_inc(up_loaded, 16)
            sp.dma_start(down_raw[:, :, :, :], down_w.rearrange("e (c p) d -> p e c d", p=P)).then_inc(down_loaded, 16)
            sp.dma_start(wrkv[:, :], w_rkv).then_inc(attw_loaded, 16)
            sp.dma_start(wo[:, :], w_o).then_inc(attw_loaded, 16)
            for t in range(BT):
                sp.dma_start(bo_row[:, t, :], b_o.rearrange("(a d) -> a d", a=1)).then_inc(attw_loaded, 16)
            for f in range(FFNS):
                for b in range(B):
                    sp.wait_ge(xn_ready, B * f + b + 1)
                    sp.dma_start(xn_tiles[f][:, BT * b:BT * (b + 1), :],
                                 xn[:, BT * b:BT * (b + 1), :]).then_inc(xn_stored, 16)
                for g in range(OUT_GROUPS):
                    sp.wait_ge(y_ready, SLOT_TILES * f + OUT_GROUP * (g + 1))
                    s = OUT_GROUP * (g % 2)
                    sp.dma_start(y_tiles[f][:, OUT_GROUP * g:OUT_GROUP * (g + 1), :],
                                 y_out[:, s:s + OUT_GROUP, :]).then_inc(y_stored[g % 2], 16)
            for b in range(B):
                sp.wait_ge(out_ready, b + 1)
                sp.dma_start(out_tiles[:, BT * b:BT * (b + 1), :],
                             x[:, BT * b:BT * (b + 1), :]).then_inc(out_stored, 16)
            sp.wait_ge(out_stored, 16 * B)

        @block.gpsimd
        def _(pool):
            step = Counter(pool, const_made)
            zeroed = step.mark(pool.memset(ident[:, :], 0.0))
            ones = step.mark(pool.memset(ones_b[:, :], 1.0))
            step.mark(pool.memset(ones_f[:, :], 1.0))
            step.after(ones)
            step.mark(pool.affine_select(out=ident[:, :], in_=ident[:, :], compare_op=ALU.not_equal, fill=1.0,
                                         base=0, pattern=[[-1, P]], channel_multiplier=1))
            step.mark(pool.affine_select(out=before[:, :], in_=ones_b[:, :], compare_op=ALU.is_gt, fill=0.0,
                                         base=0, pattern=[[1, P]], channel_multiplier=-1))
            low = dict(allow_small_or_imprecise_dtypes=True)
            step.mark(pool.iota(iota_slot[:, :], [[1, P]], base=0, channel_multiplier=0, **low))
            step.mark(pool.iota(iota_tile[:, :], [[1, SLOT_TILES]], base=0, channel_multiplier=0, **low))
            step.mark(pool.iota(iota_part[:, :], [[0, 1]], base=0, channel_multiplier=1, **low))
            step.mark(pool.iota(iota_tok_tile[:, :, :], [[P, TILES], [0, SLOT_TILES]], base=0,
                                channel_multiplier=0, **low))
            step.mark(pool.iota(rank_code[:, :, :], [[-1, E], [0, TILES]], base=E, channel_multiplier=0, **low))
            pool.wait_ge(w_hi, 1)
            pool.tensor_tensor(up_lo[:, :], up_raw.rearrange("p e h -> p (e h)"),
                               up_hi[:, :].bitcast(F32), ALU.subtract).then_inc(w_lo, 1)
            pool.wait_ge(w_hi, 2)
            pool.tensor_tensor(down_lo[:, :], down_raw[:, :, :, :].rearrange("p e c d -> p (e c d)"),
                               down_hi[:, :].bitcast(F32), ALU.subtract).then_inc(w_lo, 1)
            for f in range(FFNS):
                pool.wait_ge(route_ready, f + 1)
                pool.wait_ge(xn_stored, 16 * B * (f + 1))
                for j in range(SLOT_TILES):
                    n = SLOT_TILES * f + j
                    if n >= GATHER_BUFS:
                        pool.wait_ge(xt_transposed, n - GATHER_BUFS + 1)
                    pool.indirect_dma_start(gathered[:, n % GATHER_BUFS, :], None, xn_dram[f],
                                            bass.IndirectOffsetOnAxis(ap=src_tok[:, j:j + 1], axis=0)
                                            ).then_inc(tile_gathered[n % GATHER_BUFS], 16)
                for s in range(2):
                    groups = sum(1 for g in range(OUT_GROUPS) if g % 2 == s)
                    pool.wait_ge(y_stored[s], 16 * groups * (f + 1))
                for t in range(TILES):
                    pool.indirect_dma_start(y[:, t, :], None, y_dram[f],
                                            bass.IndirectOffsetOnAxis(ap=pos_i[:, t:t + 1], axis=0)
                                            ).then_inc(y_gathered[t // BT], 16)

        @block.scalar
        def _(act):
            step = Counter(act, act_step)
            act.wait_ge(cols_loaded, 16 * 7)
            a = step.mark(nc.scalar.activation(col_tmp[:, 0:1], nu_c, ACT.Exp))
            nc.scalar.activation(col_tmp[:, 1:2], nu_c, ACT.Exp, bias=gam_c).then_inc(act_setup, 1)
            step.after(a)
            nc.scalar.activation(lam[:, :], col_tmp[:, 0:1], ACT.Exp, scale=-1.0).then_inc(act_setup, 1)
            nc.scalar.mul(neg_br[:, :], br_c, -1.0).then_inc(act_setup, 1)
            act.wait_ge(cent_made, 1)
            nc.scalar.activation(cent_sq[:, :], cent_t[:, :], ACT.Square).then_inc(act_setup, 1)

            def transposed_copy(f, b):
                n = B * f + b
                act.wait_ge(xn_transposed, n + 1)
                if n >= 2:
                    act.wait_ge(scored, n - 1)
                nc.scalar.copy(xn_t[:, n % 2, :], (tr[1] if f else tr[n % 2])[:, :]).then_inc(xn_t_ready, 1)

            def base(f, b):
                act.wait_ge(scal_ready, B * f + b + 1)
                act.wait_ge(xn_ready, B * f + b + 1)
                for t in range(BT * b, BT * (b + 1)):
                    last = nc.scalar.activation(x[:, t, :], x[:, t, :], ACT.Identity,
                                                bias=nbias[:, 0, t:t + 1], scale=base_s[:, t:t + 1])
                last.then_inc(base_ready, 1)

            def experts(f):
                def x_hi(j):
                    n = SLOT_TILES * f + j
                    act.wait_ge(xt_transposed, n + 1)
                    if n >= XT_BUFS:
                        act.wait_ge(up_done, n - XT_BUFS + 1)
                    nc.scalar.activation(xt_hi[:, n % XT_BUFS, :], tr[n % 2][:, 0:P], ACT.Copy,
                                         scale=scale_c).then_inc(xt_hi_ready, 1)

                def gate(j):
                    n = SLOT_TILES * f + j
                    act.wait_ge(up_done, n + 1)
                    if n >= 2:
                        act.wait_ge(hid_ready, n - 1)
                    nc.scalar.activation(silu[:, n % 2, :], up_ps[n % 2][:, HID:2 * HID], ACT.Silu).then_inc(silu_ready, 1)

                def h_hi(j):
                    n = SLOT_TILES * f + j
                    act.wait_ge(ht_transposed, n + 1)
                    if n >= HT_BUFS:
                        act.wait_ge(down_done, n - HT_BUFS + 1)
                    nc.scalar.copy(ht_hi[:, n % HT_BUFS, :], ht_ps[n % 2][:, 0:2 * P]).then_inc(ht_hi_ready, 1)

                x_hi(0)
                x_hi(1)
                for j in range(SLOT_TILES + 1):
                    if j < SLOT_TILES:
                        gate(j)
                    if j + 2 < SLOT_TILES:
                        x_hi(j + 2)
                    if j >= 1:
                        h_hi(j - 1)

            for b in range(B):
                transposed_copy(0, b)
                if b == 3:
                    act.wait_ge(up_loaded, 16)
                    nc.scalar.copy(up_hi[:, :], up_raw.rearrange("p e h -> p (e h)")).then_inc(w_hi, 1)
                    act.wait_ge(down_loaded, 16)
                    nc.scalar.copy(down_hi[:, :], down_raw[:, :, :, :].rearrange("p e c d -> p (e c d)")).then_inc(w_hi, 1)
            for b in range(B):
                base(0, b)
            experts(0)

            def att_in(b):
                act.wait_ge(att_scal, b + 1)
                if b >= 2:
                    act.wait_ge(xa_transposed, b - 1)
                for t in range(BT):
                    k = BT * b + t
                    last = nc.scalar.activation(xa[:, b % 2, t, :], x[:, k, :], ACT.Identity,
                                                bias=nbias[:, 1, k:k + 1], scale=rs_val[:, 0, k:k + 1])
                last.then_inc(xa_ready, 1)

            def att_mid(b):
                act.wait_ge(xa_transposed, b + 1)
                if b >= 2:
                    act.wait_ge(rkv_done, b - 1)
                nc.scalar.copy(xa_t[:, b % 2, :], tr[0][:, :]).then_inc(xa_t_ready, 1)
                act.wait_ge(rkv_done, b + 1)
                if b >= 2:
                    act.wait_ge(gate_ready, b - 1)
                nc.scalar.activation(ex_r[:, b % 2, :], r_ps[:, :], ACT.Exp, bias=neg_br[:, :], scale=-1.0)
                nc.scalar.activation(ex_k[:, b % 2, :], k_ps[:, :], ACT.Exp, bias=bk_c).then_inc(ex_ready, 1)

            for b in range(B + 2):
                if b < B:
                    att_in(b)
                    att_mid(b)
                if b >= 2:
                    transposed_copy(1, b - 2)
                    base(1, b - 2)
            experts(1)

        @block.vector
        def _(dve):
            step = Counter(dve, dve_step)
            v = nc.vector

            def rsqrt(a, tmp, seed, val):
                step.after(step.mark(v.tensor_scalar(seed, a.bitcast(I32), 1, None, ALU.logical_shift_right)))
                step.after(step.mark(v.tensor_scalar(seed, seed, -1.0, RSQRT_SEED, ALU.mult, ALU.add)))
                cur = seed.bitcast(F32)
                for _ in range(3):
                    step.after(step.mark(v.tensor_tensor(tmp, cur, cur, ALU.mult)))
                    step.after(step.mark(v.scalar_tensor_tensor(tmp, tmp, -0.5, a, ALU.mult, ALU.mult)))
                    step.after(step.mark(v.scalar_tensor_tensor(val, tmp, 1.5, cur, ALU.add, ALU.mult)))
                    cur = val

            def moments(t0, t1):
                for t in range(t0, t1):
                    last = v.bn_stats(stats[:, t, :], x[:, t, :])
                s = stats[:, t0:t1, :]
                step.after(step.mark(last))
                step.mark(v.tensor_tensor(mean[:, t0:t1], s[:, :, 1], s[:, :, 4], ALU.add))
                step.mark(v.tensor_tensor(diff[:, t0:t1], s[:, :, 1], s[:, :, 4], ALU.subtract))
                step.after(step.mark(v.tensor_tensor(var[:, t0:t1], s[:, :, 2], s[:, :, 5], ALU.add)))
                step.mark(v.scalar_tensor_tensor(diff[:, t0:t1], diff[:, t0:t1], 0.25, diff[:, t0:t1], ALU.mult, ALU.mult))
                step.after(step.mark(v.tensor_scalar(mean[:, t0:t1], mean[:, t0:t1], 0.5, None, ALU.mult)))
                step.after(step.mark(v.scalar_tensor_tensor(var[:, t0:t1], var[:, t0:t1], 1.0 / D, diff[:, t0:t1],
                                                            ALU.mult, ALU.add)))

            def ffn_input(f, t0, t1):
                moments(t0, t1)
                a, w, sd, r = (z[:, :, t0:t1] for z in (rs_arg, rs_tmp, rs_int, rs_val))
                step.after(step.mark(v.tensor_scalar(a[:, 0, :], var[:, t0:t1], LN_EPS, None, ALU.add)))
                step.after(step.mark(v.scalar_tensor_tensor(a[:, 1, :], a[:, 0, :], RMS_EPS, var[:, t0:t1],
                                                            ALU.mult, ALU.add)))
                rsqrt(a, w, sd, r)
                if f:
                    dve.wait_ge(xa_ready, t1 // BT)
                step.mark(v.scalar_tensor_tensor(nbias[:, 0, t0:t1], mean[:, t0:t1], -0.5, r[:, 0, :], ALU.mult, ALU.mult))
                step.mark(v.tensor_scalar(base_s[:, t0:t1], r[:, 0, :], 0.5, 1.0, ALU.mult, ALU.add))
                step.after(step.mark(v.scalar_tensor_tensor(nbias[:, 1, t0:t1], mean[:, t0:t1], -1.0, r[:, 1, :],
                                                            ALU.mult, ALU.mult)))
                for b in range(t0 // BT, t1 // BT):
                    v.engine_nop().then_inc(scal_ready, 1)
                for t in range(t0, t1):
                    last = v.tensor_scalar(xn[:, t, :], x[:, t, :], rs_val[:, 1, t:t + 1], nbias[:, 1, t:t + 1],
                                           ALU.mult, ALU.add)
                    if t % BT == BT - 1:
                        last.then_inc(xn_ready, 1)

            def route(f):
                by_token = "p e t -> p t e"
                dve.wait_ge(scored, B * (f + 1))
                step.after(step.mark(v.tensor_tensor(
                    score[:, :, :].rearrange(by_token), score_ps[:, 0:TILES * E].rearrange("p (t e) -> p t e", e=E),
                    cnorm[:, :].unsqueeze(1).to_broadcast([P, TILES, E]), ALU.subtract)))
                step.after(step.mark(v.tensor_reduce(best[:, :], score[:, :, :].rearrange(by_token), axis=AX.X, op=ALU.max)))
                wide = best[:, :].unsqueeze(1).to_broadcast([P, E, TILES])
                step.after(step.mark(v.tensor_tensor(code[:, :, :], score[:, :, :], wide, ALU.is_ge)))
                step.after(step.mark(v.tensor_tensor(code[:, :, :], code[:, :, :], rank_code[:, :, :], ALU.mult)))
                step.after(step.mark(v.tensor_reduce(best[:, :], code[:, :, :].rearrange(by_token), axis=AX.X, op=ALU.max)))
                v.tensor_tensor(onehot[:, :, :], code[:, :, :], wide, ALU.is_equal).then_inc(onehot_ready, 1)
                dve.wait_ge(ranks_ready, f + 1)
                total = rank_ps[:, TILES * E:2 * TILES * E]
                csum2 = csum[:, :, :].rearrange("p e t -> p (e t)")
                slot2 = slot[:, :, :].rearrange("p e t -> p (e t)")
                step.after(step.mark(v.tensor_tensor_scan(csum2, ones_f[:, :], total, 0.0, ALU.mult, ALU.add)))
                step.mark(v.tensor_copy(starts[:, 1:E + 1], csum[:, :, TILES - 1]))
                step.after(step.mark(v.tensor_tensor(slot2, csum2, total, ALU.subtract)))
                step.mark(v.tensor_tensor(slot2, slot2, rank_ps[:, 0:TILES * E], ALU.add))
                step.after(step.mark(v.tensor_tensor(count[:, :], starts[:, 1:E + 1], starts[:, 0:E], ALU.subtract)))
                step.after(step.mark(v.tensor_scalar(tiles_i[:, :], count[:, :], float(P - 1), None, ALU.add)))
                step.after(step.mark(v.tensor_scalar(tiles_i[:, :], tiles_i[:, :], 7, None, ALU.arith_shift_right)))
                step.after(step.mark(v.tensor_copy(tiles_f[:, :], tiles_i[:, :])))
                step.after(step.mark(v.tensor_tensor_scan(tile_end[:, :], ones_f[:, 0:E], tiles_f[:, :], 0.0,
                                                          ALU.mult, ALU.add)))
                step.after(step.mark(v.tensor_tensor(pad[:, :], tile_end[:, :], tiles_f[:, :], ALU.subtract)))
                step.after(step.mark(v.scalar_tensor_tensor(pad[:, :], pad[:, :], float(P), starts[:, 0:E],
                                                            ALU.mult, ALU.subtract)))
                step.after(step.mark(v.tensor_tensor(slot[:, :, :], slot[:, :, :],
                                                     pad[:, :].unsqueeze(2).to_broadcast([P, E, TILES]), ALU.add)))
                step.after(step.mark(v.tensor_tensor(slot2, slot2, onehot[:, :, :].rearrange("p e t -> p (e t)"), ALU.mult)))
                if f:
                    dve.wait_ge(y_gathered[B - 1], 16 * BT)
                step.after(step.mark(v.tensor_reduce(pos[:, :], slot[:, :, :].rearrange(by_token), axis=AX.X, op=ALU.add)))
                step.after(step.mark(v.tensor_copy(pos_i[:, :], pos[:, :])))
                step.mark(v.tensor_scalar(hi_i[:, :], pos_i[:, :], 7, None, ALU.arith_shift_right))
                step.after(step.mark(v.tensor_scalar(lo_i[:, :], pos_i[:, :], P - 1, None, ALU.bitwise_and)))
                step.mark(v.tensor_copy(hi_f[:, :], hi_i[:, :]))
                step.after(step.mark(v.tensor_copy(lo_f[:, :], lo_i[:, :])))
                step.after(step.mark(v.tensor_tensor(
                    in_tile[:, :, :], iota_tile[:, :].unsqueeze(1).to_broadcast([P, TILES, SLOT_TILES]),
                    hi_f[:, :].unsqueeze(2).to_broadcast([P, TILES, SLOT_TILES]), ALU.is_equal)))
                step.mark(v.tensor_tensor(tok_id[:, :, 0, :], in_tile[:, :, :], iota_tok_tile[:, :, :], ALU.mult))
                step.after(step.mark(v.tensor_scalar(tok_id[:, :, 1, :], in_tile[:, :, :], iota_part[:, :], None, ALU.mult)))
                for t in range(TILES):
                    v.tensor_scalar(in_slot[:, t, :], iota_slot[:, :], lo_f[:, t:t + 1], None,
                                    ALU.is_equal).then_inc(in_slot_ready, 1)
                step.after(step.mark(v.tensor_tensor(
                    past[:, :, :], iota_tile[0:1, :].unsqueeze(2).to_broadcast([1, SLOT_TILES, E]),
                    tile_end[0:1, :].unsqueeze(1).to_broadcast([1, SLOT_TILES, E]), ALU.is_ge)))
                step.after(step.mark(v.tensor_reduce(exp_f[:, :], past[:, :, :], axis=AX.X, op=ALU.add)))
                step.after(step.mark(v.tensor_scalar(exp_i[:, :], exp_f[:, :], float(E - 1), None, ALU.min)))
                dve.wait_ge(src_summed, f + 1)
                v.tensor_copy(src_tok[:, :], tr[0][:, 0:SLOT_TILES]).then_inc(route_ready, 1)

            def experts(f):
                def x_lo(j):
                    n = SLOT_TILES * f + j
                    dve.wait_ge(xt_hi_ready, n + 1)
                    v.scalar_tensor_tensor(xt_lo[:, n % XT_BUFS, :], tr[n % 2][:, 0:P], scale_c,
                                           xt_hi[:, n % XT_BUFS, :].bitcast(F32), ALU.mult, ALU.subtract
                                           ).then_inc(xt_lo_ready, 1)

                def hidden(j):
                    n = SLOT_TILES * f + j
                    dve.wait_ge(silu_ready, n + 1)
                    if n >= 2:
                        dve.wait_ge(ht_transposed, n - 1)
                    v.tensor_tensor(hid[:, n % 2, :], up_ps[n % 2][:, 0:HID], silu[:, n % 2, :], ALU.mult).then_inc(hid_ready, 1)

                def h_lo(j):
                    n = SLOT_TILES * f + j
                    dve.wait_ge(ht_hi_ready, n + 1)
                    v.tensor_tensor(ht_lo[:, n % HT_BUFS, :], ht_ps[n % 2][:, 0:2 * P],
                                    ht_hi[:, n % HT_BUFS, :].bitcast(F32), ALU.subtract).then_inc(ht_lo_ready, 1)

                def y_copy(j):
                    n = SLOT_TILES * f + j
                    dve.wait_ge(down_done, n + 1)
                    g = j // OUT_GROUP
                    if j % OUT_GROUP == 0 and OUT_GROUPS * f + g >= 2:
                        per = [sum(1 for k in range(OUT_GROUPS) if k % 2 == s) for s in range(2)]
                        dve.wait_ge(y_stored[g % 2], 16 * (per[g % 2] * f + g // 2))
                    s = OUT_GROUP * (g % 2) + j % OUT_GROUP
                    v.tensor_copy(y_out[:, s, :], y_ps[n % 2][:, 0:D]).then_inc(y_ready, 1)

                x_lo(0)
                x_lo(1)
                for j in range(SLOT_TILES + 3):
                    if j < SLOT_TILES:
                        hidden(j)
                    if j + 2 < SLOT_TILES:
                        x_lo(j + 2)
                    if 0 <= j - 1 < SLOT_TILES:
                        h_lo(j - 1)
                    if j >= 3:
                        y_copy(j - 3)

            dve.wait_ge(pe_setup, 1)
            v.tensor_copy(cent_t[:, :], tr[0][:, 0:E]).then_inc(cent_made, 1)
            dve.wait_ge(cent_made, 1)
            dve.wait_ge(cols_loaded, 16 * 7)
            v.tensor_scalar(cent_rhs[:, :], cent_t[:, :], scale_c, 2.0, ALU.mult, ALU.mult).then_inc(dve_setup, 1)
            step.mark(v.memset(starts[:, 0:1], 0.0))
            dve.wait_ge(act_setup, 3)
            step.mark(v.tensor_scalar(gamma[:, :], col_tmp[:, 1:2], -1.0, None, ALU.add))
            dve.wait_ge(const_made, 3)
            step.mark(v.tensor_scalar(lam_row[:, 0:TILES * E], ones_f[:, :], lam[:, :], None, ALU.mult))
            step.mark(v.tensor_scalar(lam_row[:, TILES * E:L], ones_f[:, 0:L - TILES * E], lam[:, :], None, ALU.mult))
            dve.wait_ge(pe_setup, 2)
            step.mark(v.tensor_copy(cnorm[:, :], tr[1][:, 0:E]))
            for g in range(TILES // (X_GROUP * BT) ):
                for b in range(X_GROUP):
                    dve.wait_ge(x_loaded[X_GROUP * g + b], 16)
                ffn_input(0, X_GROUP * BT * g, X_GROUP * BT * (g + 1))
            dve.wait_ge(const_made, 10)
            route(0)
            experts(0)

            def attend(b):
                t0, t1 = BT * b, BT * (b + 1)
                dve.wait_ge(y_gathered[b], 16 * BT)
                dve.wait_ge(base_ready, b + 1)
                xb = x[:, t0:t1, :].rearrange("p t d -> p (t d)")
                step.after(step.mark(v.scalar_tensor_tensor(xb, y[:, t0:t1, :].rearrange("p t d -> p (t d)"), 0.5, xb,
                                                            ALU.mult, ALU.add)))
                moments(t0, t1)
                a, w, sd, r = (z[:, 0, t0:t1] for z in (rs_arg, rs_tmp, rs_int, rs_val))
                step.after(step.mark(v.tensor_scalar(a, var[:, t0:t1], LN_EPS, None, ALU.add)))
                rsqrt(a, w, sd, r)
                v.scalar_tensor_tensor(nbias[:, 1, t0:t1], mean[:, t0:t1], -1.0, r, ALU.mult, ALU.mult).then_inc(att_scal, 1)

            def scan(b):
                k = ex_k[:, b % 2, :]
                dve.wait_ge(ex_ready, b + 1)
                one = step.mark(v.scalar_tensor_tensor(kv[:, :], v_ps[:, :], bv_c, k, ALU.add, ALU.mult))
                step.mark(v.tensor_tensor_scan(u_k[:, :], lam_row[:, :], k, 0.0, ALU.mult, ALU.add))
                step.after(one)
                v.engine_nop().then_inc(kv_ready, 1)
                step.mark(v.tensor_scalar(gk[:, b % 2, :], k, gamma[:, :], DEN_EPS, ALU.mult, ALU.add))
                step.after(step.mark(v.tensor_tensor_scan(u_kv[:, :], lam_row[:, :], kv[:, :], 0.0, ALU.mult, ALU.add)))
                step.mark(v.tensor_tensor(u_k[:, :], u_k[:, :], gk[:, b % 2, :], ALU.add))
                step.after(step.mark(v.scalar_tensor_tensor(kv[:, :], kv[:, :], gamma[:, :], u_kv[:, :], ALU.mult, ALU.add)))
                step.after(step.mark(v.scalar_tensor_tensor(u_k[:, :], ex_r[:, b % 2, :], 1.0, u_k[:, :], ALU.add, ALU.mult)))
                step.after(step.mark(v.reciprocal(u_k[:, :], u_k[:, :])))
                if b >= 2:
                    dve.wait_ge(att_done, b - 1)
                v.tensor_tensor(gate_t[:, b % 2, :], kv[:, :], u_k[:, :], ALU.mult).then_inc(gate_ready, 1)

            def finish(b):
                t0, t1 = BT * b, BT * (b + 1)
                xb = x[:, t0:t1, :].rearrange("p t d -> p (t d)")
                dve.wait_ge(att_done, b + 1)
                step.after(step.mark(v.tensor_tensor(xb, xb, att_ps[:, :], ALU.add)))
                v.engine_nop().then_inc(x2_ready, 1)
                ffn_input(1, t0, t1)

            for b in range(B + 2):
                if b < B:
                    attend(b)
                if 1 <= b <= B:
                    scan(b - 1)
                if b >= 2:
                    finish(b - 2)
            route(1)
            experts(1)
            for b in range(B):
                dve.wait_ge(y_gathered[b], 2 * 16 * BT)
                dve.wait_ge(base_ready, B + b + 1)
                xb = x[:, BT * b:BT * (b + 1), :].rearrange("p t d -> p (t d)")
                v.scalar_tensor_tensor(xb, y[:, BT * b:BT * (b + 1), :].rearrange("p t d -> p (t d)"), 0.5, xb,
                                       ALU.mult, ALU.add).then_inc(out_ready, 1)

        @block.tensor
        def _(pe):
            mm = nc.tensor.matmul
            pe.wait_ge(const_made, 4)
            pe.wait_ge(cols_loaded, 16 * 7)
            nc.tensor.transpose(tr[0][:, 0:E], cent[:, :], ident[0:E, 0:E]).then_inc(pe_setup, 1)
            pe.wait_ge(act_setup, 4)
            mm(tr[1][:, 0:E], ones_f[:, 0:P], cent_sq[:, :], start=True, stop=True).then_inc(pe_setup, 1)

            def xn_transpose(f, b):
                n = B * f + b
                pe.wait_ge(xn_ready, n + 1)
                if f:
                    pe.wait_ge(xn_t_ready, n)
                elif n >= 2:
                    pe.wait_ge(xn_t_ready, n - 1)
                for t in range(BT):
                    last = nc.tensor.transpose((tr[1] if f else tr[n % 2])[:, t * P:(t + 1) * P], xn[:, BT * b + t, :], ident[:, :])
                last.then_inc(xn_transposed, 1)

            def score_batch(f, b):
                n = B * f + b
                pe.wait_ge(xn_t_ready, n + 1)
                for t in range(BT):
                    k = BT * b + t
                    last = mm(score_ps[:, k * E:(k + 1) * E], xn_t[:, n % 2, t * P:(t + 1) * P], cent_rhs[:, :],
                              start=True, stop=True)
                last.then_inc(scored, 1)

            def ranks(f):
                hot = onehot[:, :, :].rearrange("p e t -> p (e t)")
                pe.wait_ge(onehot_ready, f + 1)
                mm(rank_ps[:, 0:TILES * E], before[:, :], hot, start=True, stop=True)
                mm(rank_ps[:, TILES * E:2 * TILES * E], ones_b[:, :], hot, start=True, stop=True).then_inc(ranks_ready, 1)
                for t in range(TILES):
                    pe.wait_ge(in_slot_ready, TILES * f + t + 1)
                    for part in range(2):
                        last = mm(tr[0][:, 0:SLOT_TILES], in_slot[:, t, :], tok_id[:, t, part, :],
                                  start=t + part == 0, stop=t + part == TILES)
                last.then_inc(src_summed, 1)

            def experts(f):
                expert = {}

                def x_t(j):
                    n = SLOT_TILES * f + j
                    pe.wait_ge(tile_gathered[n % GATHER_BUFS], 16 * (n // GATHER_BUFS + 1))
                    if n >= 2:
                        pe.wait_ge(xt_lo_ready, n - 1)
                    nc.tensor.transpose(tr[n % 2][:, 0:P], gathered[:, n % GATHER_BUFS, :], ident[:, :]).then_inc(xt_transposed, 1)
                    expert[j] = pe.value_load(exp_i[0:1, j:j + 1], min_val=0, max_val=E - 1)

                def up(j):
                    n = SLOT_TILES * f + j
                    pe.wait_ge(xt_lo_ready, n + 1)
                    if n >= 2:
                        pe.wait_ge(hid_ready, n - 1)
                    h, lo = (z[:, n % XT_BUFS, :] for z in (xt_hi, xt_lo))
                    at = bass.ds(expert[j] * (2 * HID), 2 * HID)
                    mm(up_ps[n % 2][:, :], h, up_hi[:, at], start=True, stop=False)
                    mm(up_ps[n % 2][:, :], h, up_lo[:, at], start=False, stop=False)
                    mm(up_ps[n % 2][:, :], lo, up_hi[:, at], start=False, stop=True).then_inc(up_done, 1)

                def h_t(j):
                    n = SLOT_TILES * f + j
                    pe.wait_ge(hid_ready, n + 1)
                    if n >= 2:
                        pe.wait_ge(ht_lo_ready, n - 1)
                    for c in range(2):
                        last = nc.tensor.transpose(ht_ps[n % 2][:, c * P:(c + 1) * P], hid[:, n % 2, c * P:(c + 1) * P],
                                                   ident[:, :])
                    last.then_inc(ht_transposed, 1)

                def down(j):
                    n = SLOT_TILES * f + j
                    pe.wait_ge(ht_lo_ready, n + 1)
                    if n >= 2:
                        pe.wait_ge(y_ready, n - 1)
                    for c in range(2):
                        h, lo = (z[:, n % HT_BUFS, c * P:(c + 1) * P] for z in (ht_hi, ht_lo))
                        at = bass.ds(expert[j] * (2 * D) + c * D, D)
                        mm(y_ps[n % 2][:, 0:D], h, down_hi[:, at], start=c == 0, stop=False)
                        mm(y_ps[n % 2][:, 0:D], h, down_lo[:, at], start=False, stop=False)
                        last = mm(y_ps[n % 2][:, 0:D], lo, down_hi[:, at], start=False, stop=c == 1)
                    last.then_inc(down_done, 1)

                pe.wait_ge(route_ready, f + 1)
                x_t(0)
                x_t(1)
                pe.wait_ge(w_lo, 2)
                for j in range(SLOT_TILES + 3):
                    if j < SLOT_TILES:
                        up(j)
                    if j + 2 < SLOT_TILES:
                        x_t(j + 2)
                    if 0 <= j - 1 < SLOT_TILES:
                        h_t(j - 1)
                    if j >= 3:
                        down(j - 3)

            pe.wait_ge(dve_setup, 1)
            for b in range(B):
                xn_transpose(0, b)
                if b >= 1:
                    score_batch(0, b - 1)
            score_batch(0, B - 1)
            ranks(0)
            experts(0)

            def project(b):
                pe.wait_ge(xa_ready, b + 1)
                if b >= 1:
                    pe.wait_ge(xa_t_ready, b)
                for t in range(BT):
                    last = nc.tensor.transpose(tr[0][:, t * P:(t + 1) * P], xa[:, b % 2, t, :], ident[:, :])
                last.then_inc(xa_transposed, 1)
                pe.wait_ge(xa_t_ready, b + 1)
                if b >= 1:
                    pe.wait_ge(ex_ready, b)
                    pe.wait_ge(kv_ready, b)
                for i, bank in enumerate((r_ps, k_ps, v_ps)):
                    last = mm(bank[:, :], wrkv[:, i * P:(i + 1) * P], xa_t[:, b % 2, :], start=True, stop=True)
                last.then_inc(rkv_done, 1)

            def att_out(b):
                pe.wait_ge(gate_ready, b + 1)
                if b >= 1:
                    pe.wait_ge(x2_ready, b)
                for t in range(BT):
                    o = att_ps[:, t * D:(t + 1) * D]
                    mm(o, ones_f[0:1, 0:P], bo_row[0:1, t, :], start=True, stop=False)
                    last = mm(o, gate_t[:, b % 2, t * P:(t + 1) * P], wo[:, :], start=False, stop=True)
                last.then_inc(att_done, 1)

            pe.wait_ge(attw_loaded, 16 * (2 + BT))
            for b in range(B + 2):
                if b < B:
                    project(b)
                if 1 <= b <= B:
                    att_out(b - 1)
                if b >= 2:
                    xn_transpose(1, b - 2)
                    score_batch(1, b - 2)
            ranks(1)
            experts(1)


_INS = ['L0_attn_inputs', 'L0_attn_W_rkv', 'L0_attn_b_rkv', 'L0_attn_W_o', 'L0_attn_b_o', 'L0_attn_nu_log',
        'L0_attn_gamma_log', 'L0_ffn_scale', 'L0_ffn_centroids', 'L0_ffn_up_w', 'L0_ffn_down_w']


def kernel(**inputs):
    import concourse.bacc as _bacc
    from concourse.bass_utils import run_bass_kernel_spmd as _run

    nc = _bacc.Bacc("TRN2", target_bir_lowering=False, num_devices=1)
    arrays, args = {}, []
    for name in _INS:
        a = np.ascontiguousarray(inputs[name])
        arrays[f"in_{name}"] = a
        args.append(nc.dram_tensor(f"in_{name}", a.shape, mybir.dt.from_np(a.dtype), kind="ExternalInput").ap())
    out = nc.dram_tensor("out", (B, L, D), F32, kind="ExternalOutput").ap()
    macaron(nc, *args, out)
    r = _run(nc, [arrays], core_ids=[0])
    return r.results[0]["out"]
```

```python
import concourse.bass as bass
import numpy as np
from concourse import mybir
from contextlib import ExitStack

F32 = mybir.dt.float32
F32R = mybir.dt.float32r
BF16 = mybir.dt.bfloat16
I32 = mybir.dt.int32
ALU = mybir.AluOpType
ACT = mybir.ActivationFunctionType
AX = mybir.AxisListType

P = 128
B, L, D = 8, 512, 128
E, HID = 8, 256
TOKENS = B * L
TILES = TOKENS // P
BT = L // P
SLOT_TILES = TILES + E - 1
FFNS = 2
LN_EPS, RMS_EPS, DEN_EPS = 1e-5, 1e-6, 1e-6

GATHER_BUFS = 6
XT_BUFS = 3
HT_BUFS = 3
HID_BUFS = 3
OUT_GROUP = 3
OUT_BUFS = 2 * OUT_GROUP
OUT_GROUPS = SLOT_TILES // OUT_GROUP
X_GROUPS = 4
X_TILES = TILES // X_GROUPS
DEPTH = 5


class Counter:

    def __init__(self, engine, sem):
        self.engine, self.sem, self.n = engine, sem, 0

    def mark(self, instruction):
        instruction.then_inc(self.sem, 1)
        self.n += 1
        return self.n

    def after(self, n):
        self.engine.wait_ge(self.sem, n)


def macaron(nc, x_in, w_rkv, b_rkv, w_o, b_o, nu_log, gamma_log, ffn_scale, centroids, up_w, down_w, out):
    xn_dram = [nc.dram_tensor(f"xn_scratch_{f}", (TOKENS, D), F32, kind="Internal").ap() for f in range(FFNS)]
    y_dram = [nc.dram_tensor(f"y_scratch_{f}", (SLOT_TILES * P, D), F32, kind="Internal").ap() for f in range(FFNS)]

    x_tiles = x_in.rearrange("b (t p) d -> p (b t) d", p=P)
    out_tiles = out.rearrange("b (t p) d -> p (b t) d", p=P)
    xn_tiles = [a.rearrange("(t p) d -> p t d", p=P) for a in xn_dram]
    y_tiles = [a.rearrange("(t p) d -> p t d", p=P) for a in y_dram]

    with ExitStack() as ctx:
        def sb(name, shape, dt=F32):
            return ctx.enter_context(nc.sbuf_tensor(name, shape, dt))

        def pb(name):
            return ctx.enter_context(nc.psum_tensor(name, [P, 512], F32))

        def sem(name):
            return ctx.enter_context(nc.semaphore(name))

        x = sb("x", [P, TILES, D])
        xn = sb("xn", [P, TILES, D])
        up_raw = sb("up_raw", [P, E, 2 * HID])
        down_raw = sb("down_raw", [P, E, 2, D])
        up_hi = sb("up_hi", [P, E * 2 * HID], F32R)
        up_lo = sb("up_lo", [P, E * 2 * HID], F32R)
        down_half = sb("down_half", [P, E * 2 * D])
        wrkv = sb("wrkv", [D, 3 * P])
        wo = sb("wo", [P, D])
        den_eps = sb("den_eps", [P, 1])
        bo_row = sb("bo_row", [1, BT * D])
        bo_hi = sb("bo_hi", [1, BT * D], F32R)
        bo_lo = sb("bo_lo", [1, BT * D], F32R)
        ones_r = sb("ones_r", [1, P], F32R)
        cent = sb("cent", [E, D])
        cent_t = sb("cent_t", [D, E])
        cent_sq = sb("cent_sq", [D, E])
        cent_rhs = sb("cent_rhs", [D, E])
        cnorm = sb("cnorm", [P, E])
        cols = sb("cols", [P, 8])
        nu_c, gam_c, scale_c, br_c, bk_c, bv_c = (cols[:, i:i + 1] for i in range(6))
        lam = sb("lam", [P, 1])
        gamma = sb("gamma", [P, 1])
        neg_br = sb("neg_br", [P, 1])
        col_tmp = sb("col_tmp", [P, 2])
        lam_row = sb("lam_row", [P, L])
        ident = sb("ident", [P, P])
        ones_f = sb("ones_f", [P, TILES * E])
        ones_b = sb("ones_b", [P, P], BF16)
        before = sb("before", [P, P], BF16)
        iota_slot = sb("iota_slot", [P, P], BF16)
        iota_tile = sb("iota_tile", [P, SLOT_TILES])
        iota_tok_tile = sb("iota_tok_tile", [P, TILES, SLOT_TILES], BF16)
        iota_part = sb("iota_part", [P, 1])
        rank_code = sb("rank_code", [P, E, TILES])

        def row_stats(name, kinds, n):
            return {"n": n, "kinds": kinds, "stats": sb(f"{name}_stats", [P, kinds, n, 6]),
                    **{k: sb(f"{name}_{k}", [P, kinds, n]) for k in ("mean", "diff", "var")},
                    **{k: sb(f"{name}_{k}", [P, kinds + 1, n]) for k in ("arg", "log", "tmp", "val", "bias")}}

        first_rows = [row_stats(f"first{g}", 1, X_TILES) for g in range(X_GROUPS)]
        rows = [row_stats(f"rows{i}", 2, BT) for i in range(2)]
        base_s = sb("base_s", [P, TILES])
        base_b = sb("base_b", [P, TILES])
        xn_t = sb("xn_t", [D, 2, L])

        score = sb("score", [P, E, TILES])
        best = sb("best", [P, TILES])
        code = sb("code", [P, E, TILES])
        onehot = sb("onehot", [P, E, TILES], BF16)
        csum = sb("csum", [P, E, TILES])
        slot = sb("slot", [P, E, TILES])
        starts = sb("starts", [P, E + 1])
        count = sb("count", [P, E])
        tiles_i = sb("tiles_i", [P, E], I32)
        tiles_f = sb("tiles_f", [P, E])
        tile_end = sb("tile_end", [P, E])
        pad = sb("pad", [P, E])
        pos = sb("pos", [P, TILES])
        pos_i = sb("pos_i", [P, TILES], I32)
        hi_i = sb("hi_i", [P, TILES], I32)
        lo_i = sb("lo_i", [P, TILES], I32)
        hi_f = sb("hi_f", [P, TILES])
        lo_f = sb("lo_f", [P, TILES])
        in_tile = sb("in_tile", [P, TILES, SLOT_TILES], BF16)
        tok_id = sb("tok_id", [P, TILES, 2, SLOT_TILES], BF16)
        in_slot = sb("in_slot", [P, TILES, P], BF16)
        src_tok = sb("src_tok", [P, SLOT_TILES], I32)
        past = sb("past", [1, SLOT_TILES, E])
        exp_f = sb("exp_f", [1, SLOT_TILES])
        exp_i = sb("exp_i", [1, SLOT_TILES], I32)

        gathered = sb("gathered", [P, GATHER_BUFS, D])
        xt_hi = sb("xt_hi", [P, XT_BUFS, P], F32R)
        xt_lo = sb("xt_lo", [P, XT_BUFS, P], F32R)
        silu = sb("silu", [P, 2, HID])
        hid = sb("hid", [P, HID_BUFS, HID])
        ht = sb("ht", [P, HT_BUFS, 2 * P])
        y_out = sb("y_out", [P, OUT_BUFS, D])

        xa = sb("xa", [P, 2, BT, D])
        xa_t = sb("xa_t", [D, 2, L])
        ex_r = sb("ex_r", [P, L])
        ex_r1 = up_raw[:, 0:2, :]
        ex_k = up_raw[:, 2:4, :]
        gk = up_raw[:, 4:6, :]
        kv = sb("kv", [P, L])
        u_kv = sb("u_kv", [P, L])
        u_k = up_raw[:, 6:8, :]
        num = sb("num", [P, 2, L])
        den = sb("den", [P, L])
        den_r = sb("den_r", [P, 2, L])
        inv = sb("inv", [P, 2, L])
        gate_t = sb("gate_t", [P, 2, L])

        tr = [pb(f"tr{i}") for i in range(2)]
        up_ps = [pb(f"up_ps{i}") for i in range(2)]
        ht_ps = [pb(f"ht_ps{i}") for i in range(2)]
        y_ps = [pb(f"y_ps{i}") for i in range(2)]
        score_ps, rank_ps = y_ps
        r_ps, k_ps, v_ps, att_ps = up_ps[0], up_ps[1], (ht_ps[0], rank_ps), ht_ps[1]

        x_loaded = [sem(f"x_loaded{b}") for b in range(B)]
        cols_loaded = sem("cols_loaded")
        attw_loaded = sem("attw_loaded")
        up_loaded = sem("up_loaded")
        down_loaded = sem("down_loaded")
        const_made = sem("const_made")
        cent_made = sem("cent_made")
        pe_setup = sem("pe_setup")
        act_setup = sem("act_setup")
        dve_setup = sem("dve_setup")
        up_hi_ready = sem("up_hi_ready")
        up_lo_ready = sem("up_lo_ready")
        down_ready = sem("down_ready")
        dve_step = sem("dve_step")
        act_step = sem("act_step")
        args_ready = sem("args_ready")
        seed_ready = sem("seed_ready")
        rows_ready = sem("rows_ready")
        xn_ready = sem("xn_ready")
        xn_act_ready = sem("xn_act_ready")
        xn_stored = sem("xn_stored")
        xn_transposed = sem("xn_transposed")
        xn_t_ready = sem("xn_t_ready")
        scored = sem("scored")
        base_ready = sem("base_ready")
        onehot_ready = sem("onehot_ready")
        ranks_ready = sem("ranks_ready")
        in_slot_ready = sem("in_slot_ready")
        src_summed = sem("src_summed")
        route_ready = sem("route_ready")
        tile_gathered = [sem(f"tile_gathered{i}") for i in range(GATHER_BUFS)]
        xt_transposed = sem("xt_transposed")
        xt_hi_ready = sem("xt_hi_ready")
        xt_lo_ready = sem("xt_lo_ready")
        up_done = sem("up_done")
        silu_ready = sem("silu_ready")
        hid_ready = sem("hid_ready")
        ht_transposed = sem("ht_transposed")
        ht_ready = sem("ht_ready")
        down_done = sem("down_done")
        y_ready = sem("y_ready")
        y_stored = [sem(f"y_stored{i}") for i in range(2)]
        y_gathered = [sem(f"y_gathered{b}") for b in range(B)]
        xa_ready = sem("xa_ready")
        xa_transposed = sem("xa_transposed")
        xa_t_ready = sem("xa_t_ready")
        rkv_done = sem("rkv_done")
        rk_read = sem("rk_read")
        ex_ready = sem("ex_ready")
        kv_ready = sem("kv_ready")
        u_k_ready = sem("u_k_ready")
        den_ready = sem("den_ready")
        inv_ready = sem("inv_ready")
        gate_ready = sem("gate_ready")
        att_done = sem("att_done")
        x2_ready = sem("x2_ready")
        out_stored = sem("out_stored")

        block = ctx.enter_context(nc.Block())

        @block.sync
        def _(sp):
            for b in range(B):
                sp.dma_start(x[:, BT * b:BT * (b + 1), :], x_tiles[:, BT * b:BT * (b + 1), :]).then_inc(x_loaded[b], 16)
            sp.dma_start(up_raw[:, :, :], up_w.rearrange("e d h -> d e h")).then_inc(up_loaded, 16)
            sp.dma_start(down_raw[:, :, :, :], down_w.rearrange("e (c p) d -> p e c d", p=P)).then_inc(down_loaded, 16)
            sp.dma_start(wrkv[:, :], w_rkv).then_inc(attw_loaded, 16)
            sp.dma_start(wo[:, :], w_o).then_inc(attw_loaded, 16)
            for t in range(BT):
                sp.dma_start(bo_row[:, t * D:(t + 1) * D], b_o.rearrange("(a d) -> a d", a=1)).then_inc(attw_loaded, 16)
            for f in range(FFNS):
                for b in range(B):
                    sp.wait_ge(xn_ready, B * f + b + 1)
                    if f == 0:
                        sp.wait_ge(xn_act_ready, b + 1)
                    sp.dma_start(xn_tiles[f][:, BT * b:BT * (b + 1), :],
                                 xn[:, BT * b:BT * (b + 1), :]).then_inc(xn_stored, 16)
                for g in range(OUT_GROUPS):
                    sp.wait_ge(y_ready, SLOT_TILES * f + OUT_GROUP * (g + 1))
                    s = OUT_GROUP * (g % 2)
                    sp.dma_start(y_tiles[f][:, OUT_GROUP * g:OUT_GROUP * (g + 1), :],
                                 y_out[:, s:s + OUT_GROUP, :]).then_inc(y_stored[g % 2], 16)
            for b in range(B):
                sp.wait_ge(y_gathered[b], 2 * 16 * BT)
                sp.dma_start(out_tiles[:, BT * b:BT * (b + 1), :],
                             x[:, BT * b:BT * (b + 1), :]).then_inc(out_stored, 16)
            sp.wait_ge(out_stored, 16 * B)

        @block.gpsimd
        def _(pool):
            step = Counter(pool, const_made)
            zeroed = step.mark(pool.memset(ident[:, :], 0.0))
            ones = step.mark(pool.memset(ones_b[:, :], 1.0))
            step.mark(pool.memset(ones_f[:, :], 1.0))
            step.after(ones)
            step.mark(pool.affine_select(out=ident[:, :], in_=ident[:, :], compare_op=ALU.not_equal, fill=1.0,
                                         base=0, pattern=[[-1, P]], channel_multiplier=1))
            step.mark(pool.affine_select(out=before[:, :], in_=ones_b[:, :], compare_op=ALU.is_gt, fill=0.0,
                                         base=0, pattern=[[1, P]], channel_multiplier=-1))
            low = dict(allow_small_or_imprecise_dtypes=True)
            step.mark(pool.iota(iota_slot[:, :], [[1, P]], base=0, channel_multiplier=0, **low))
            step.mark(pool.iota(iota_tile[:, :], [[1, SLOT_TILES]], base=0, channel_multiplier=0, **low))
            step.mark(pool.iota(iota_part[:, :], [[0, 1]], base=0, channel_multiplier=1, **low))
            step.mark(pool.iota(iota_tok_tile[:, :, :], [[P, TILES], [0, SLOT_TILES]], base=0,
                                channel_multiplier=0, **low))
            step.mark(pool.iota(rank_code[:, :, :], [[-1, E], [0, TILES]], base=E, channel_multiplier=0, **low))
            pool.wait_ge(up_hi_ready, 1)
            pool.tensor_tensor(up_lo[:, :], up_raw[:, :, :].rearrange("p e h -> p (e h)"),
                               up_hi[:, :].bitcast(F32), ALU.subtract).then_inc(up_lo_ready, 1)

            def gather_y(f, t):
                if t % BT == 0:
                    pool.wait_ge(base_ready, B * f + t // BT + 1)
                pool.indirect_dma_start(x[:, t, :], None, y_dram[f],
                                        bass.IndirectOffsetOnAxis(ap=pos_i[:, t:t + 1], axis=0),
                                        compute_op=ALU.add).then_inc(y_gathered[t // BT], 16)

            def denominator(b):
                pool.wait_ge(u_k_ready, b + 1)
                pool.wait_ge(ex_ready, b + 1)
                step.after(step.mark(pool.tensor_tensor(den[:, :], u_k[:, b % 2, :], gk[:, b % 2, :], ALU.add)))
                if b >= 2:
                    pool.wait_ge(inv_ready, b - 1)
                pool.tensor_tensor(den_r[:, b % 2, :], den[:, :], ex_r1[:, b % 2, :], ALU.mult).then_inc(den_ready, 1)

            def gated(b):
                pool.wait_ge(inv_ready, b + 1)
                if b >= 2:
                    pool.wait_ge(att_done, b - 1)
                pool.tensor_tensor(gate_t[:, b % 2, :], num[:, b % 2, :], inv[:, b % 2, :], ALU.mult).then_inc(gate_ready, 1)

            for f in range(FFNS):
                pool.wait_ge(route_ready, f + 1)
                pool.wait_ge(xn_stored, 16 * B * (f + 1))
                for j in range(SLOT_TILES):
                    n = SLOT_TILES * f + j
                    if n >= GATHER_BUFS:
                        pool.wait_ge(xt_transposed, n - GATHER_BUFS + 1)
                    pool.indirect_dma_start(gathered[:, n % GATHER_BUFS, :], None, xn_dram[f],
                                            bass.IndirectOffsetOnAxis(ap=src_tok[:, j:j + 1], axis=0)
                                            ).then_inc(tile_gathered[n % GATHER_BUFS], 16)
                for s in range(2):
                    groups = sum(1 for g in range(OUT_GROUPS) if g % 2 == s)
                    pool.wait_ge(y_stored[s], 16 * groups * (f + 1))
                if f == 1:
                    for t in range(TILES):
                        gather_y(f, t)
                else:
                    for t in range(BT):
                        gather_y(f, t)
                    for i in range(B + 2):
                        if i + 1 < B:
                            gather_y(f, BT * (i + 1))
                            gather_y(f, BT * (i + 1) + 1)
                        if i >= 2:
                            denominator(i - 2)
                        if i + 1 < B:
                            gather_y(f, BT * (i + 1) + 2)
                            gather_y(f, BT * (i + 1) + 3)
                        if i >= 2:
                            gated(i - 2)

        @block.scalar
        def _(act):
            step = Counter(act, act_step)
            act.dma_start(cent[:, :], centroids).then_inc(cols_loaded, 16)
            for src, dst in ((ffn_scale, scale_c), (nu_log, nu_c), (gamma_log, gam_c),
                             (b_rkv[0:P], br_c), (b_rkv[P:2 * P], bk_c), (b_rkv[2 * P:3 * P], bv_c)):
                act.dma_start(dst, src.rearrange("(p a) -> p a", a=1)).then_inc(cols_loaded, 16)
            act.wait_ge(cols_loaded, 16 * 7)
            act.preload_act_table_set("natural_log_exp_and_others")
            a = step.mark(nc.scalar.activation(col_tmp[:, 0:1], nu_c, ACT.Exp))
            nc.scalar.activation(col_tmp[:, 1:2], nu_c, ACT.Exp, bias=gam_c).then_inc(act_setup, 1)
            step.after(a)
            nc.scalar.activation(lam[:, :], col_tmp[:, 0:1], ACT.Exp, scale=-1.0).then_inc(act_setup, 1)
            nc.scalar.mul(neg_br[:, :], br_c, -1.0).then_inc(act_setup, 1)

            def transposed_copy(f, b):
                n = B * f + b
                act.wait_ge(xn_transposed, n + 1)
                if n >= 2:
                    act.wait_ge(scored, n - 1)
                nc.scalar.copy(xn_t[:, n % 2, :], (tr[1] if f else tr[n % 2])[:, :]).then_inc(xn_t_ready, 1)

            def base(f, b):
                act.wait_ge(xn_ready, B * f + b + 1)
                for t in range(BT * b, BT * (b + 1)):
                    last = nc.scalar.activation(x[:, t, :], x[:, t, :], ACT.Identity,
                                                bias=base_b[:, t:t + 1], scale=base_s[:, t:t + 1])
                last.then_inc(base_ready, 1)

            def seed(n, r):
                act.wait_ge(args_ready, n + 1)
                step.after(step.mark(nc.scalar.activation(r["log"][:, :, :], r["arg"][:, :, :], ACT.Ln)))
                nc.scalar.activation(r["val"][:, :, :], r["log"][:, :, :], ACT.Exp, scale=-0.5).then_inc(seed_ready, 1)

            def experts(f):
                def x_hi(j):
                    n = SLOT_TILES * f + j
                    act.wait_ge(xt_transposed, n + 1)
                    if n >= XT_BUFS:
                        act.wait_ge(up_done, n - XT_BUFS + 1)
                    nc.scalar.activation(xt_hi[:, n % XT_BUFS, :], tr[n % 2][:, 0:P], ACT.Copy,
                                         scale=scale_c).then_inc(xt_hi_ready, 1)

                def gate(j):
                    n = SLOT_TILES * f + j
                    act.wait_ge(up_done, n + 1)
                    if n >= 2:
                        act.wait_ge(hid_ready, n - 1)
                    nc.scalar.activation(silu[:, n % 2, :], up_ps[n % 2][:, HID:2 * HID], ACT.Silu).then_inc(silu_ready, 1)

                def h_copy(j):
                    n = SLOT_TILES * f + j
                    act.wait_ge(ht_transposed, n + 1)
                    if n >= HT_BUFS:
                        act.wait_ge(down_done, n - HT_BUFS + 1)
                    nc.scalar.copy(ht[:, n % HT_BUFS, :], ht_ps[n % 2][:, 0:2 * P]).then_inc(ht_ready, 1)

                x_hi(0)
                x_hi(1)
                for j in range(SLOT_TILES + 2):
                    if j < SLOT_TILES:
                        gate(j)
                    if j + 2 < SLOT_TILES:
                        x_hi(j + 2)
                    if j >= 2:
                        h_copy(j - 2)

            for g in range(X_GROUPS):
                seed(g, first_rows[g])
                act.wait_ge(rows_ready, g + 1)
                r = first_rows[g]
                for i in range(1, X_TILES, 2):
                    t = X_TILES * g + i
                    last = nc.scalar.activation(xn[:, t, :], x[:, t, :], ACT.Identity,
                                                bias=r["bias"][:, 1, i:i + 1], scale=r["val"][:, 1, i:i + 1])
                    if t % BT == BT - 1:
                        last.then_inc(xn_act_ready, 1)
                if g == 0:
                    act.wait_ge(cent_made, 1)
                    nc.scalar.activation(cent_sq[:, :], cent_t[:, :], ACT.Square).then_inc(act_setup, 1)
                for b in range(X_TILES // BT * (g - 1), X_TILES // BT * g):
                    if b >= 0:
                        transposed_copy(0, b)
            for b in range(B - X_TILES // BT, B):
                transposed_copy(0, b)
            act.wait_ge(up_loaded, 16)
            nc.scalar.copy(up_hi[:, :], up_raw[:, :, :].rearrange("p e h -> p (e h)")).then_inc(up_hi_ready, 1)
            act.wait_ge(down_loaded, 16)
            nc.scalar.mul(down_half[:, :], down_raw[:, :, :, :].rearrange("p e c d -> p (e c d)"), 0.5).then_inc(down_ready, 1)
            act.preload_act_table_set("silu_and_others")
            experts(0)
            act.preload_act_table_set("natural_log_exp_and_others")
            for b in range(B):
                base(0, b)

            def keys(b):
                act.wait_ge(rkv_done, b + 1)
                if b >= 2:
                    act.wait_ge(kv_ready, b - 1)
                    act.wait_ge(u_k_ready, b - 1)
                    act.wait_ge(den_ready, b - 1)
                a = step.mark(nc.scalar.activation(ex_k[:, b % 2, :], k_ps[:, :], ACT.Exp, bias=bk_c))
                if b >= 1:
                    act.wait_ge(ex_ready, b)
                nc.scalar.activation(ex_r[:, :], r_ps[:, :], ACT.Exp, bias=neg_br[:, :], scale=-1.0).then_inc(rk_read, 1)
                return a

            def keys_rest(b, a):
                step.after(a)
                nc.scalar.activation(gk[:, b % 2, :], ex_k[:, b % 2, :], ACT.Identity, bias=den_eps[:, :], scale=gamma[:, :])
                act.wait_ge(rk_read, b + 1)
                nc.scalar.activation(ex_r1[:, b % 2, :], ex_r[:, :], ACT.Identity, bias=1.0).then_inc(ex_ready, 1)

            def normalise(i):
                r = rows[i % 2]
                act.wait_ge(rows_ready, X_GROUPS + i + 1)
                if i < B:
                    if i >= 2:
                        act.wait_ge(xa_transposed, i - 1)
                    for t in range(BT):
                        last = nc.scalar.activation(xa[:, i % 2, t, :], x[:, BT * i + t, :], ACT.Identity,
                                                    bias=r["bias"][:, 0, t:t + 1], scale=r["val"][:, 0, t:t + 1])
                    last.then_inc(xa_ready, 1)

            def normalise_ffn(i):
                if i >= DEPTH:
                    r = rows[i % 2]
                    b = i - DEPTH
                    for t in range(BT):
                        last = nc.scalar.activation(xn[:, BT * b + t, :], x[:, BT * b + t, :], ACT.Identity,
                                                    bias=r["bias"][:, 2, t:t + 1], scale=r["val"][:, 2, t:t + 1])
                    last.then_inc(xn_ready, 1)

            for i in range(B + DEPTH):
                seed(X_GROUPS + i, rows[i % 2])
                normalise(i)
                if 1 <= i <= B:
                    exps = keys(i - 1)
                if i < B:
                    act.wait_ge(xa_transposed, i + 1)
                    if i >= 2:
                        act.wait_ge(rkv_done, i - 1)
                    nc.scalar.copy(xa_t[:, i % 2, :], tr[0][:, :]).then_inc(xa_t_ready, 1)
                if 1 <= i <= B:
                    keys_rest(i - 1, exps)
                if i > DEPTH:
                    transposed_copy(1, i - DEPTH - 1)
                normalise_ffn(i)
            transposed_copy(1, B - 1)
            act.preload_act_table_set("silu_and_others")
            experts(1)
            for b in range(B):
                base(1, b)

        @block.vector
        def _(dve):
            step = Counter(dve, dve_step)
            v = nc.vector

            def row_moments(r, k, i, t):
                return v.bn_stats(r["stats"][:, k, i, :], x[:, t, :])

            def rows_1(r, after):
                s = r["stats"]
                step.after(after)
                step.mark(v.tensor_tensor(r["mean"][:, :, :], s[:, :, :, 1], s[:, :, :, 4], ALU.add))
                step.mark(v.tensor_tensor(r["diff"][:, :, :], s[:, :, :, 1], s[:, :, :, 4], ALU.subtract))
                return step.mark(v.tensor_tensor(r["var"][:, :, :], s[:, :, :, 2], s[:, :, :, 5], ALU.add))

            def rows_2(r, after):
                step.after(after)
                step.mark(v.tensor_scalar(r["mean"][:, :, :], r["mean"][:, :, :], 0.5, None, ALU.mult))
                return step.mark(v.scalar_tensor_tensor(r["diff"][:, :, :], r["diff"][:, :, :], 0.25, r["diff"][:, :, :],
                                                        ALU.mult, ALU.mult))

            def rows_3(r, after):
                step.after(after)
                return step.mark(v.scalar_tensor_tensor(r["var"][:, :, :], r["var"][:, :, :], 1.0 / D, r["diff"][:, :, :],
                                                        ALU.mult, ALU.add))

            def rows_4(r, after):
                step.after(after)
                return step.mark(v.tensor_scalar(r["arg"][:, 0:r["kinds"], :], r["var"][:, :, :], LN_EPS, None, ALU.add))

            def rows_5(r, after):
                k = r["kinds"]
                step.after(after)
                v.scalar_tensor_tensor(r["arg"][:, k, :], r["arg"][:, k - 1, :], RMS_EPS, r["var"][:, k - 1, :],
                                       ALU.mult, ALU.add).then_inc(args_ready, 1)

            def rows_6(n, r):
                dve.wait_ge(seed_ready, n + 1)
                return step.mark(v.tensor_tensor(r["tmp"][:, :, :], r["val"][:, :, :], r["val"][:, :, :], ALU.mult))

            def rows_7(r, after):
                step.after(after)
                return step.mark(v.scalar_tensor_tensor(r["tmp"][:, :, :], r["tmp"][:, :, :], -0.5, r["arg"][:, :, :],
                                                        ALU.mult, ALU.mult))

            def rows_8(r, after):
                step.after(after)
                return step.mark(v.scalar_tensor_tensor(r["val"][:, :, :], r["tmp"][:, :, :], 1.5, r["val"][:, :, :],
                                                        ALU.add, ALU.mult))

            def rows_9(r, t0, after):
                k, n = r["kinds"], r["n"]
                step.after(after)
                if k > 1:
                    step.mark(v.scalar_tensor_tensor(r["bias"][:, 0, :], r["mean"][:, 0, :], -1.0, r["val"][:, 0, :],
                                                     ALU.mult, ALU.mult))
                if t0 is not None:
                    step.mark(v.tensor_scalar(base_s[:, t0:t0 + n], r["val"][:, k - 1, :], 0.5, 1.0, ALU.mult, ALU.add))
                    step.mark(v.scalar_tensor_tensor(base_b[:, t0:t0 + n], r["mean"][:, k - 1, :], -0.5,
                                                     r["val"][:, k - 1, :], ALU.mult, ALU.mult))
                v.scalar_tensor_tensor(r["bias"][:, k, :], r["mean"][:, k - 1, :], -1.0, r["val"][:, k, :],
                                       ALU.mult, ALU.mult).then_inc(rows_ready, 1)

            def route(f):
                by_token = "p e t -> p t e"
                dve.wait_ge(scored, B * (f + 1))
                step.after(step.mark(v.tensor_tensor(
                    score[:, :, :].rearrange(by_token), score_ps[:, 0:TILES * E].rearrange("p (t e) -> p t e", e=E),
                    cnorm[:, :].unsqueeze(1).to_broadcast([P, TILES, E]), ALU.subtract)))
                step.after(step.mark(v.tensor_reduce(best[:, :], score[:, :, :].rearrange(by_token), axis=AX.X, op=ALU.max)))
                wide = best[:, :].unsqueeze(1).to_broadcast([P, E, TILES])
                step.after(step.mark(v.tensor_tensor(code[:, :, :], score[:, :, :], wide, ALU.is_ge)))
                step.after(step.mark(v.tensor_tensor(code[:, :, :], code[:, :, :], rank_code[:, :, :], ALU.mult)))
                step.after(step.mark(v.tensor_reduce(best[:, :], code[:, :, :].rearrange(by_token), axis=AX.X, op=ALU.max)))
                v.tensor_tensor(onehot[:, :, :], code[:, :, :], wide, ALU.is_equal).then_inc(onehot_ready, 1)
                dve.wait_ge(ranks_ready, f + 1)
                total = rank_ps[:, TILES * E:2 * TILES * E]
                csum2 = csum[:, :, :].rearrange("p e t -> p (e t)")
                slot2 = slot[:, :, :].rearrange("p e t -> p (e t)")
                step.after(step.mark(v.tensor_tensor_scan(csum2, ones_f[:, :], total, 0.0, ALU.mult, ALU.add)))
                step.mark(v.tensor_copy(starts[:, 1:E + 1], csum[:, :, TILES - 1]))
                step.after(step.mark(v.tensor_tensor(slot2, csum2, total, ALU.subtract)))
                step.mark(v.tensor_tensor(slot2, slot2, rank_ps[:, 0:TILES * E], ALU.add))
                step.after(step.mark(v.tensor_tensor(count[:, :], starts[:, 1:E + 1], starts[:, 0:E], ALU.subtract)))
                step.after(step.mark(v.tensor_scalar(tiles_i[:, :], count[:, :], float(P - 1), None, ALU.add)))
                step.after(step.mark(v.tensor_scalar(tiles_i[:, :], tiles_i[:, :], 7, None, ALU.arith_shift_right)))
                step.after(step.mark(v.tensor_copy(tiles_f[:, :], tiles_i[:, :])))
                step.after(step.mark(v.tensor_tensor_scan(tile_end[:, :], ones_f[:, 0:E], tiles_f[:, :], 0.0,
                                                          ALU.mult, ALU.add)))
                step.after(step.mark(v.tensor_tensor(pad[:, :], tile_end[:, :], tiles_f[:, :], ALU.subtract)))
                step.after(step.mark(v.scalar_tensor_tensor(pad[:, :], pad[:, :], float(P), starts[:, 0:E],
                                                            ALU.mult, ALU.subtract)))
                step.after(step.mark(v.tensor_tensor(slot[:, :, :], slot[:, :, :],
                                                     pad[:, :].unsqueeze(2).to_broadcast([P, E, TILES]), ALU.add)))
                step.after(step.mark(v.tensor_tensor(slot2, slot2, onehot[:, :, :].rearrange("p e t -> p (e t)"), ALU.mult)))
                step.after(step.mark(v.tensor_reduce(pos[:, :], slot[:, :, :].rearrange(by_token), axis=AX.X, op=ALU.add)))
                step.after(step.mark(v.tensor_copy(pos_i[:, :], pos[:, :])))
                step.mark(v.tensor_scalar(hi_i[:, :], pos_i[:, :], 7, None, ALU.arith_shift_right))
                step.after(step.mark(v.tensor_scalar(lo_i[:, :], pos_i[:, :], P - 1, None, ALU.bitwise_and)))
                step.mark(v.tensor_copy(hi_f[:, :], hi_i[:, :]))
                step.after(step.mark(v.tensor_copy(lo_f[:, :], lo_i[:, :])))
                step.after(step.mark(v.tensor_tensor(
                    in_tile[:, :, :], iota_tile[:, :].unsqueeze(1).to_broadcast([P, TILES, SLOT_TILES]),
                    hi_f[:, :].unsqueeze(2).to_broadcast([P, TILES, SLOT_TILES]), ALU.is_equal)))
                step.mark(v.tensor_tensor(tok_id[:, :, 0, :], in_tile[:, :, :], iota_tok_tile[:, :, :], ALU.mult))
                step.after(step.mark(v.tensor_scalar(tok_id[:, :, 1, :], in_tile[:, :, :], iota_part[:, :], None, ALU.mult)))
                for t in range(TILES):
                    v.tensor_scalar(in_slot[:, t, :], iota_slot[:, :], lo_f[:, t:t + 1], None,
                                    ALU.is_equal).then_inc(in_slot_ready, 1)
                step.after(step.mark(v.tensor_tensor(
                    past[:, :, :], iota_tile[0:1, :].unsqueeze(2).to_broadcast([1, SLOT_TILES, E]),
                    tile_end[0:1, :].unsqueeze(1).to_broadcast([1, SLOT_TILES, E]), ALU.is_ge)))
                step.after(step.mark(v.tensor_reduce(exp_f[:, :], past[:, :, :], axis=AX.X, op=ALU.add)))
                step.after(step.mark(v.tensor_scalar(exp_i[:, :], exp_f[:, :], float(E - 1), None, ALU.min)))
                dve.wait_ge(src_summed, f + 1)
                v.tensor_copy(src_tok[:, :], tr[0][:, 0:SLOT_TILES]).then_inc(route_ready, 1)

            def experts(f):
                def x_lo(j):
                    n = SLOT_TILES * f + j
                    dve.wait_ge(xt_hi_ready, n + 1)
                    v.scalar_tensor_tensor(xt_lo[:, n % XT_BUFS, :], tr[n % 2][:, 0:P], scale_c,
                                           xt_hi[:, n % XT_BUFS, :].bitcast(F32), ALU.mult, ALU.subtract
                                           ).then_inc(xt_lo_ready, 1)

                def hidden(j):
                    n = SLOT_TILES * f + j
                    dve.wait_ge(silu_ready, n + 1)
                    if n >= HID_BUFS:
                        dve.wait_ge(ht_transposed, n - HID_BUFS + 1)
                    v.tensor_tensor(hid[:, n % HID_BUFS, :], up_ps[n % 2][:, 0:HID], silu[:, n % 2, :], ALU.mult).then_inc(hid_ready, 1)

                def y_copy(j):
                    n = SLOT_TILES * f + j
                    dve.wait_ge(down_done, n + 1)
                    g = j // OUT_GROUP
                    if j % OUT_GROUP == 0 and OUT_GROUPS * f + g >= 2:
                        per = [sum(1 for k in range(OUT_GROUPS) if k % 2 == s) for s in range(2)]
                        dve.wait_ge(y_stored[g % 2], 16 * (per[g % 2] * f + g // 2))
                    s = OUT_GROUP * (g % 2) + j % OUT_GROUP
                    v.tensor_copy(y_out[:, s, :], y_ps[n % 2][:, 0:D]).then_inc(y_ready, 1)

                x_lo(0)
                x_lo(1)
                for j in range(SLOT_TILES + 3):
                    if j < SLOT_TILES:
                        hidden(j)
                    if j + 2 < SLOT_TILES:
                        x_lo(j + 2)
                    if j >= 3:
                        y_copy(j - 3)

            def set_up():
                dve.wait_ge(pe_setup, 1)
                v.tensor_copy(cent_t[:, :], rank_ps[:, 0:E]).then_inc(cent_made, 1)
                dve.wait_ge(cent_made, 1)
                dve.wait_ge(cols_loaded, 16 * 7)
                v.tensor_scalar(cent_rhs[:, :], cent_t[:, :], scale_c, 2.0, ALU.mult, ALU.mult).then_inc(dve_setup, 1)
                step.mark(v.memset(starts[:, 0:1], 0.0))
                dve.wait_ge(act_setup, 3)
                step.mark(v.tensor_scalar(gamma[:, :], col_tmp[:, 1:2], -1.0, None, ALU.add))
                dve.wait_ge(const_made, 3)
                step.mark(v.tensor_scalar(lam_row[:, 0:TILES * E], ones_f[:, :], lam[:, :], None, ALU.mult))
                step.mark(v.tensor_scalar(lam_row[:, TILES * E:L], ones_f[:, 0:L - TILES * E], lam[:, :], None, ALU.mult))

            def first_moments(g, i):
                t = X_TILES * g + i
                if t % BT == 0:
                    dve.wait_ge(x_loaded[t // BT], 16)
                return row_moments(first_rows[g], 0, i, t)

            def first_rest(g, after, between):
                r = first_rows[g]
                a = rows_1(r, after)
                between(2)
                a = rows_2(r, a)
                between(1)
                a = rows_3(r, a)
                between(1)
                a = rows_4(r, a)
                between(1)
                rows_5(r, a)
                between(3)
                a = rows_6(g, r)
                a = rows_7(r, a)
                a = rows_8(r, a)
                rows_9(r, X_TILES * g, a)
                dve.wait_ge(rows_ready, g + 1)
                for i in range(0, X_TILES, 2):
                    t = X_TILES * g + i
                    last = v.tensor_scalar(xn[:, t, :], x[:, t, :], r["val"][:, 1, i:i + 1], r["bias"][:, 1, i:i + 1],
                                           ALU.mult, ALU.add)
                    if t % BT == BT - 2:
                        last.then_inc(xn_ready, 1)

            for r in rows:
                last = v.memset(r["stats"][:, :, :, :], 1.0)
            step.mark(last)
            v.memset(den_eps[:, :], DEN_EPS).then_inc(dve_setup, 1)
            done = 0
            for i in range(X_TILES):
                done = step.mark(first_moments(0, i))
            for g in range(X_GROUPS):
                ahead = []

                def next_moments(n):
                    if g + 1 < X_GROUPS:
                        for _ in range(n):
                            ahead.append(step.mark(first_moments(g + 1, len(ahead))))

                first_rest(g, done, next_moments)
                if g == 0:
                    set_up()
                if ahead:
                    done = ahead[-1]
            dve.wait_ge(const_made, 10)
            dve.wait_ge(pe_setup, 2)
            step.after(step.mark(v.tensor_copy(cnorm[:, :], rank_ps[:, E:2 * E])))
            route(0)
            experts(0)

            dve.wait_ge(attw_loaded, 16 * (2 + BT))
            step.mark(v.tensor_copy(ones_r[:, :], ones_f[0:1, 0:P]))
            part = step.mark(v.tensor_copy(bo_hi[:, :], bo_row[:, :]))
            step.after(part)
            v.tensor_tensor(bo_lo[:, :], bo_row[:, :], bo_hi[:, :].bitcast(F32), ALU.subtract).then_inc(dve_setup, 1)

            xv = x[:, :, :].rearrange("p t d -> p (t d)")
            moments_done = 0
            for i in range(B + DEPTH):
                r = rows[i % 2]
                s = i - 2 if 2 <= i < B + 2 else None
                o = i - 4 if 4 <= i < B + 4 else None
                if i < B:
                    dve.wait_ge(y_gathered[i], 16 * BT)
                    for t in range(BT):
                        last = row_moments(r, 0, t, BT * i + t)
                    moments_done = step.mark(last)
                if s is not None:
                    k = ex_k[:, s % 2, :]
                    dve.wait_ge(ex_ready, s + 1)
                    v.scalar_tensor_tensor(kv[:, :], v_ps[s % 2][:, :], bv_c, k, ALU.add, ALU.mult).then_inc(kv_ready, 1)
                a = rows_1(r, moments_done)
                if s is not None:
                    if s >= 2:
                        dve.wait_ge(den_ready, s - 1)
                    v.tensor_tensor_scan(u_k[:, s % 2, :], lam_row[:, :], k, 0.0, ALU.mult, ALU.add).then_inc(u_k_ready, 1)
                a = rows_2(r, a)
                if s is not None:
                    dve.wait_ge(kv_ready, s + 1)
                    scanned = step.mark(v.tensor_tensor_scan(u_kv[:, :], lam_row[:, :], kv[:, :], 0.0, ALU.mult, ALU.add))
                a = rows_3(r, a)
                a = rows_4(r, a)
                if s is not None:
                    step.after(scanned)
                    if s >= 2:
                        dve.wait_ge(gate_ready, s - 1)
                    numed = step.mark(v.scalar_tensor_tensor(num[:, s % 2, :], kv[:, :], gamma[:, :], u_kv[:, :],
                                                             ALU.mult, ALU.add))
                rows_5(r, a)
                if o is not None:
                    xb = xv[:, L * o:L * (o + 1)]
                    dve.wait_ge(att_done, o + 1)
                    dve.wait_ge(xa_ready, o + 1)
                    v.tensor_tensor(xb, xb, att_ps[:, :], ALU.add).then_inc(x2_ready, 1)
                a = rows_6(X_GROUPS + i, r)
                if o is not None:
                    nxt = rows[(i + 1) % 2]
                    dve.wait_ge(x2_ready, o + 1)
                    for t in range(BT):
                        last = row_moments(nxt, 1, t, BT * o + t)
                    moments_done = step.mark(last)
                a = rows_7(r, a)
                a = rows_8(r, a)
                if s is not None:
                    dve.wait_ge(den_ready, s + 1)
                rows_9(r, BT * (i - DEPTH) if i >= DEPTH else None, a)
                if s is not None:
                    v.reciprocal(inv[:, s % 2, :], den_r[:, s % 2, :]).then_inc(inv_ready, 1)
            route(1)
            experts(1)

        @block.tensor
        def _(pe):
            mm = nc.tensor.matmul
            pe.wait_ge(const_made, 4)
            pe.wait_ge(cols_loaded, 16 * 7)
            nc.tensor.transpose(rank_ps[:, 0:E], cent[:, :], ident[0:E, 0:E]).then_inc(pe_setup, 1)

            def xn_transpose(f, b):
                n = B * f + b
                pe.wait_ge(xn_ready, n + 1)
                if f == 0:
                    pe.wait_ge(xn_act_ready, b + 1)
                if f:
                    pe.wait_ge(xn_t_ready, n)
                elif n >= 2:
                    pe.wait_ge(xn_t_ready, n - 1)
                for t in range(BT):
                    last = nc.tensor.transpose((tr[1] if f else tr[n % 2])[:, t * P:(t + 1) * P], xn[:, BT * b + t, :], ident[:, :])
                last.then_inc(xn_transposed, 1)

            def score_batch(f, b):
                n = B * f + b
                pe.wait_ge(xn_t_ready, n + 1)
                for t in range(BT):
                    k = BT * b + t
                    last = mm(score_ps[:, k * E:(k + 1) * E], xn_t[:, n % 2, t * P:(t + 1) * P], cent_rhs[:, :],
                              start=True, stop=True)
                last.then_inc(scored, 1)

            def ranks(f):
                hot = onehot[:, :, :].rearrange("p e t -> p (e t)")
                pe.wait_ge(onehot_ready, f + 1)
                mm(rank_ps[:, 0:TILES * E], before[:, :], hot, start=True, stop=True)
                mm(rank_ps[:, TILES * E:2 * TILES * E], ones_b[:, :], hot, start=True, stop=True).then_inc(ranks_ready, 1)
                for t in range(TILES):
                    pe.wait_ge(in_slot_ready, TILES * f + t + 1)
                    for part in range(2):
                        last = mm(tr[0][:, 0:SLOT_TILES], in_slot[:, t, :], tok_id[:, t, part, :],
                                  start=t + part == 0, stop=t + part == TILES)
                last.then_inc(src_summed, 1)

            def load_expert(j):
                return nc.values_load(exp_i[0:1, j:j + 1], engines=(mybir.EngineType.PE,), min_val=0, max_val=E - 1,
                                      skip_runtime_bounds_check_because="a count of experts, cut at the last one")

            def experts(f):
                expert = {}

                def x_t(j):
                    n = SLOT_TILES * f + j
                    pe.wait_ge(tile_gathered[n % GATHER_BUFS], 16 * (n // GATHER_BUFS + 1))
                    if n >= 2:
                        pe.wait_ge(xt_lo_ready, n - 1)
                    nc.tensor.transpose(tr[n % 2][:, 0:P], gathered[:, n % GATHER_BUFS, :], ident[:, :]).then_inc(xt_transposed, 1)

                def up(j):
                    n = SLOT_TILES * f + j
                    pe.wait_ge(xt_lo_ready, n + 1)
                    if n >= 2:
                        pe.wait_ge(hid_ready, n - 1)
                    h, lo = (z[:, n % XT_BUFS, :] for z in (xt_hi, xt_lo))
                    at = bass.ds(expert[j] * (2 * HID), 2 * HID)
                    mm(up_ps[n % 2][:, :], h, up_hi[:, at], start=True, stop=False)
                    mm(up_ps[n % 2][:, :], h, up_lo[:, at], start=False, stop=False)
                    mm(up_ps[n % 2][:, :], lo, up_hi[:, at], start=False, stop=True).then_inc(up_done, 1)
                    if j + 2 < SLOT_TILES:
                        expert[j + 2] = load_expert(j + 2)

                def h_t(j):
                    n = SLOT_TILES * f + j
                    pe.wait_ge(hid_ready, n + 1)
                    if n >= 2:
                        pe.wait_ge(ht_ready, n - 1)
                    for c in range(2):
                        last = nc.tensor.transpose(ht_ps[n % 2][:, c * P:(c + 1) * P], hid[:, n % HID_BUFS, c * P:(c + 1) * P],
                                                   ident[:, :])
                    last.then_inc(ht_transposed, 1)

                def down(j):
                    n = SLOT_TILES * f + j
                    pe.wait_ge(ht_ready, n + 1)
                    if n >= 2:
                        pe.wait_ge(y_ready, n - 1)
                    for c in range(2):
                        at = bass.ds(expert[j] * (2 * D) + c * D, D)
                        last = mm(y_ps[n % 2][:, 0:D], ht[:, n % HT_BUFS, c * P:(c + 1) * P], down_half[:, at],
                                  start=c == 0, stop=c == 1)
                    last.then_inc(down_done, 1)

                pe.wait_ge(route_ready, f + 1)
                for j in range(2):
                    expert[j] = load_expert(j)
                x_t(0)
                x_t(1)
                pe.wait_ge(up_lo_ready, 1)
                pe.wait_ge(down_ready, 1)
                for j in range(SLOT_TILES + 3):
                    if j < SLOT_TILES:
                        up(j)
                    if j >= 3:
                        down(j - 3)
                    if j + 2 < SLOT_TILES:
                        x_t(j + 2)
                    if 0 <= j - 2 < SLOT_TILES:
                        h_t(j - 2)

            for b in range(B):
                xn_transpose(0, b)
                if b == 1:
                    pe.wait_ge(dve_setup, 2)
                    pe.wait_ge(act_setup, 4)
                    mm(rank_ps[:, E:2 * E], ones_f[:, 0:P], cent_sq[:, :], start=True, stop=True).then_inc(pe_setup, 1)
                if b >= 1:
                    score_batch(0, b - 1)
            score_batch(0, B - 1)
            ranks(0)
            experts(0)

            def xa_transpose(b):
                pe.wait_ge(xa_ready, b + 1)
                if b >= 1:
                    pe.wait_ge(xa_t_ready, b)
                for t in range(BT):
                    last = nc.tensor.transpose(tr[0][:, t * P:(t + 1) * P], xa[:, b % 2, t, :], ident[:, :])
                last.then_inc(xa_transposed, 1)

            def project(b):
                pe.wait_ge(xa_t_ready, b + 1)
                if b >= 1:
                    pe.wait_ge(rk_read, b)
                if b >= 2:
                    pe.wait_ge(kv_ready, b - 1)
                for i, bank in enumerate((r_ps, k_ps, v_ps[b % 2])):
                    last = mm(bank[:, :], wrkv[:, i * P:(i + 1) * P], xa_t[:, b % 2, :], start=True, stop=True)
                last.then_inc(rkv_done, 1)

            def att_out(b):
                pe.wait_ge(gate_ready, b + 1)
                if b >= 1:
                    pe.wait_ge(x2_ready, b)
                mm(att_ps[:, :], ones_r[:, :], bo_hi[:, :], start=True, stop=False)
                mm(att_ps[:, :], ones_r[:, :], bo_lo[:, :], start=False, stop=False)
                for t in range(BT):
                    last = mm(att_ps[:, t * D:(t + 1) * D], gate_t[:, b % 2, t * P:(t + 1) * P], wo[:, :], start=False, stop=t == BT - 1)
                last.then_inc(att_done, 1)

            pe.wait_ge(attw_loaded, 16 * (2 + BT))
            pe.wait_ge(dve_setup, 3)
            for i in range(B + DEPTH):
                if i < B:
                    xa_transpose(i)
                if 3 <= i < B + 3:
                    att_out(i - 3)
                if i > DEPTH:
                    xn_transpose(1, i - DEPTH - 1)
                if i < B:
                    project(i)
                if i > DEPTH:
                    score_batch(1, i - DEPTH - 1)
            xn_transpose(1, B - 1)
            score_batch(1, B - 1)
            ranks(1)
            experts(1)


_INS = ['L0_attn_inputs', 'L0_attn_W_rkv', 'L0_attn_b_rkv', 'L0_attn_W_o', 'L0_attn_b_o', 'L0_attn_nu_log',
        'L0_attn_gamma_log', 'L0_ffn_scale', 'L0_ffn_centroids', 'L0_ffn_up_w', 'L0_ffn_down_w']


def kernel(**inputs):
    import concourse.bacc as _bacc
    from concourse.bass_utils import run_bass_kernel_spmd as _run

    nc = _bacc.Bacc("TRN2", target_bir_lowering=False, num_devices=1)
    arrays, args = {}, []
    for name in _INS:
        a = np.ascontiguousarray(inputs[name])
        arrays[f"in_{name}"] = a
        args.append(nc.dram_tensor(f"in_{name}", a.shape, mybir.dt.from_np(a.dtype), kind="ExternalInput").ap())
    out = nc.dram_tensor("out", (B, L, D), F32, kind="ExternalOutput").ap()
    macaron(nc, *args, out)
    r = _run(nc, [arrays], core_ids=[0])
    return r.results[0]["out"]
```

```python
import concourse.bass as bass
import numpy as np
from concourse import mybir
from contextlib import ExitStack

F32 = mybir.dt.float32
F32R = mybir.dt.float32r
BF16 = mybir.dt.bfloat16
I32 = mybir.dt.int32
ALU = mybir.AluOpType
ACT = mybir.ActivationFunctionType
AX = mybir.AxisListType

P = 128
B, L, D = 8, 512, 128
E, HID = 8, 256
TOKENS = B * L
TILES = TOKENS // P
BT = L // P
SLOT_TILES = TILES + E - 1
FFNS = 2
LN_EPS, RMS_EPS, DEN_EPS = 1e-5, 1e-6, 1e-6

ROUND = 1.5 * 2.0 ** 23

GATHER_BUFS = 7
GATHER2_BUFS = TILES // 2
FILL = 3
DVE_SUMS = 2
SCATTER_LAG = 12
XT_BUFS = 3
HT_BUFS = 4
Y_AHEAD = 2
DOWN_LAG = 4
HID_BUFS = 3
OUT_GROUP = 3
OUT_BUFS = 2 * OUT_GROUP
OUT_GROUPS = SLOT_TILES // OUT_GROUP
X_GROUPS = 4
X_TILES = TILES // X_GROUPS
ACT_BATCHES = 5
DEPTH = 5


class Counter:

    def __init__(self, engine, sem):
        self.engine, self.sem, self.n = engine, sem, 0

    def mark(self, instruction):
        instruction.then_inc(self.sem, 1)
        self.n += 1
        return self.n

    def after(self, n):
        self.engine.wait_ge(self.sem, n)


def macaron(nc, x_in, w_rkv, b_rkv, w_o, b_o, nu_log, gamma_log, ffn_scale, centroids, up_w, down_w, out):
    xn_dram = [nc.dram_tensor(f"xn_scratch_{f}", (TOKENS, (f + 1) * D), F32, kind="Internal").ap() for f in range(FFNS)]
    y_dram = nc.dram_tensor("y_scratch", (SLOT_TILES * P, D), F32, kind="Internal").ap()

    x_tiles = x_in.rearrange("b (t p) d -> p (b t) d", p=P)
    out_rows = out.rearrange("b l d -> (b l) d")
    xn_tiles = [a.rearrange("(t p) d -> p t d", p=P) for a in xn_dram]
    y_tiles = y_dram.rearrange("(t p) d -> p t d", p=P)

    with ExitStack() as ctx:
        def sb(name, shape, dt=F32):
            return ctx.enter_context(nc.sbuf_tensor(name, shape, dt))

        def pb(name):
            return ctx.enter_context(nc.psum_tensor(name, [P, 512], F32))

        def sem(name):
            return ctx.enter_context(nc.semaphore(name))

        x = sb("x", [P, TILES, D])
        xn = sb("xn", [P, TILES, D])
        up_raw = sb("up_raw", [P, E, 2 * HID])
        down_raw = sb("down_raw", [P, E, 2, D])
        up_hi = sb("up_hi", [P, E * 2 * HID], F32R)
        up_lo = sb("up_lo", [P, E * 2 * HID], F32R)
        down_half = sb("down_half", [P, E * 2 * D])
        wrkv = sb("wrkv", [D, 3 * P])
        wo = sb("wo", [P, D])
        den_eps = sb("den_eps", [P, 1])
        bo_row = sb("bo_row", [1, BT * D])
        bo_hi = sb("bo_hi", [1, BT * D], F32R)
        bo_lo = sb("bo_lo", [1, BT * D], F32R)
        ones_r = sb("ones_r", [1, P], F32R)
        cent = sb("cent", [E, D])
        cent_t = sb("cent_t", [D, E])
        cent_sq = sb("cent_sq", [D, E])
        cent_rhs = sb("cent_rhs", [D, E])
        cnorm = sb("cnorm", [P, E])
        cols = sb("cols", [P, 8])
        nu_c, gam_c, scale_c, br_c, bk_c, bv_c = (cols[:, i:i + 1] for i in range(6))
        lam = sb("lam", [P, 1])
        gamma = sb("gamma", [P, 1])
        neg_br = sb("neg_br", [P, 1])
        col_tmp = sb("col_tmp", [P, 2])
        lam_row = sb("lam_row", [P, L])
        ident = sb("ident", [P, P])
        ones_f = sb("ones_f", [P, TILES * E])
        ones_b = sb("ones_b", [P, P], BF16)
        not_before = sb("not_before", [P, P], BF16)
        iota_slot = sb("iota_slot", [P, P, X_TILES], BF16)
        iota_tile = sb("iota_tile", [P, SLOT_TILES, TILES], BF16)
        iota_tok_tile = sb("iota_tok_tile", [P, TILES], BF16)
        no_token = sb("no_token", [P, 1])
        iota_part = sb("iota_part", [P, 1])
        within = sb("within", [P, E, TILES])
        rank_code = sb("rank_code", [P, E, TILES])

        def row_stats(name, kinds, n):
            return {"n": n, "kinds": kinds, "stats": sb(f"{name}_stats", [P, kinds, n, 6]),
                    **{k: sb(f"{name}_{k}", [P, kinds, n]) for k in ("mean", "diff", "var")},
                    **{k: sb(f"{name}_{k}", [P, kinds + 1, n]) for k in ("arg", "log", "tmp", "val", "bias")}}

        first_rows = [row_stats(f"first{g}", 1, X_TILES) for g in range(X_GROUPS)]
        rows = [row_stats(f"rows{i}", 2, BT) for i in range(2)]
        base_s = sb("base_s", [P, TILES])
        base_b = sb("base_b", [P, TILES])
        xn_t = sb("xn_t", [D, 2, L])

        score = sb("score", [P, E, TILES])
        best = sb("best", [P, TILES])
        code = sb("code", [P, E, TILES])
        onehot = sb("onehot", [P, E, TILES], BF16)
        csum = sb("csum", [P, E, TILES])
        slot = sb("slot", [P, E, TILES])
        tile_start = sb("tile_start", [P, E])
        tiles_f = sb("tiles_f", [P, E])
        tile_end = sb("tile_end", [P, E])
        pos = sb("pos", [P, TILES])
        hi_f = sb("hi_f", [P, TILES])
        pos_i = sb("pos_i", [P, TILES], I32)
        hi = sb("hi", [P, TILES], BF16)
        lo = sb("lo", [P, TILES], BF16)
        in_tile = sb("in_tile", [P, SLOT_TILES, TILES], BF16)
        tok_id = sb("tok_id", [P, 2 * SLOT_TILES, TILES], BF16)
        in_slot = sb("in_slot", [P, X_GROUPS, P, X_TILES], BF16)
        src_sum = sb("src_sum", [P, SLOT_TILES])
        src_tok = sb("src_tok", [P, SLOT_TILES], I32)
        empty = sb("empty", [P, SLOT_TILES])
        out_tok = sb("out_tok", [P, SLOT_TILES], I32)
        past = sb("past", [1, SLOT_TILES, E])
        exp_f = sb("exp_f", [1, SLOT_TILES])
        exp_i = sb("exp_i", [1, SLOT_TILES], I32)

        gathered = sb("gathered", [P, GATHER_BUFS, D])
        xt_hi = sb("xt_hi", [P, XT_BUFS, P], F32R)
        xt_lo = sb("xt_lo", [P, XT_BUFS, P], F32R)
        silu = sb("silu", [P, 2, HID])
        hid = sb("hid", [P, HID_BUFS, HID])
        ht = sb("ht", [P, HT_BUFS, 2 * P])
        y_out = sb("y_out", [P, OUT_BUFS, D])

        gathered2 = x[:, :, :].rearrange("p (n k) d -> p n (k d)", k=2)

        def slot_rows(f, j):
            return gathered2[:, j % GATHER2_BUFS, 0:D] if f else gathered[:, j % GATHER_BUFS, :]

        def out_buf(j):
            return xn[:, j, :] if j < TILES else gathered[:, j - TILES, :]

        xa = sb("xa", [P, 2, BT, D])
        xa_t = sb("xa_t", [D, 2, L])
        ex_r = sb("ex_r", [P, L])
        ex_r1 = up_raw[:, 0:2, :]
        ex_k = up_raw[:, 2:4, :]
        gk = up_raw[:, 4:6, :]
        kv = sb("kv", [P, L])
        u_kv = sb("u_kv", [P, 2, L])
        u_k = up_raw[:, 6:8, :]
        num = sb("num", [P, 2, L])
        den = sb("den", [P, L])
        den_r = sb("den_r", [P, 2, L])
        inv = sb("inv", [P, 2, L])
        gate_t = sb("gate_t", [P, 2, L])

        tr = [pb(f"tr{i}") for i in range(2)]
        up_ps = [pb(f"up_ps{i}") for i in range(2)]
        ht_ps = [pb(f"ht_ps{i}") for i in range(2)]
        y_ps = [pb(f"y_ps{i}") for i in range(2)]
        rank_ps = y_ps[1]
        score_ps = [[y_ps[0]] * 2 + [up_ps[0]] * 2 + [up_ps[1]] * 2 + [ht_ps[0], ht_ps[1]],
                    [y_ps[0]] * 4 + [up_ps[0]] * 3 + [up_ps[1]]]
        r_ps, k_ps, v_ps, att_ps = up_ps[0], up_ps[1], (ht_ps[0], rank_ps), ht_ps[1]

        x_loaded = [sem(f"x_loaded{b}") for b in range(B)]
        cent_loaded = sem("cent_loaded")
        cols_loaded = sem("cols_loaded")
        attw_loaded = sem("attw_loaded")
        up_loaded = sem("up_loaded")
        down_loaded = sem("down_loaded")
        const_made = sem("const_made")
        cent_made = sem("cent_made")
        cent_squared = sem("cent_squared")
        pe_setup = sem("pe_setup")
        act_setup = sem("act_setup")
        dve_setup = sem("dve_setup")
        up_hi_ready = sem("up_hi_ready")
        up_lo_ready = sem("up_lo_ready")
        down_ready = sem("down_ready")
        dve_step = sem("dve_step")
        act_step = sem("act_step")
        args_ready = sem("args_ready")
        seed_ready = sem("seed_ready")
        rows_ready = sem("rows_ready")
        moments_ready = sem("moments_ready")
        xn_ready = sem("xn_ready")
        xn_act_ready = sem("xn_act_ready")
        xn_pool_ready = sem("xn_pool_ready")
        xn_stored = sem("xn_stored")
        xn_transposed = sem("xn_transposed")
        xn_t_ready = sem("xn_t_ready")
        scored = sem("scored")
        base_ready = sem("base_ready")
        onehot_ready = sem("onehot_ready")
        ranks_ready = sem("ranks_ready")
        in_slot_ready = sem("in_slot_ready")
        src_summed = sem("src_summed")
        route_ready = sem("route_ready")
        experts_ready = sem("experts_ready")
        lo_ready = sem("lo_ready")
        in_tile_ready = sem("in_tile_ready")
        tok_part_ready = sem("tok_part_ready")
        tile_gathered = [sem(f"tile_gathered{i}") for i in range(GATHER_BUFS)]
        tile_gathered2 = [sem(f"tile_gathered2_{i}") for i in range(GATHER2_BUFS)]
        base2_ready = sem("base2_ready")
        out_tok_ready = sem("out_tok_ready")
        xt_transposed = sem("xt_transposed")
        xt_hi_ready = sem("xt_hi_ready")
        xt_lo_ready = sem("xt_lo_ready")
        up_done = sem("up_done")
        silu_ready = sem("silu_ready")
        hid_ready = sem("hid_ready")
        ht_transposed = sem("ht_transposed")
        ht_ready = sem("ht_ready")
        down_done = sem("down_done")
        y_ready = sem("y_ready")
        y_stored = [sem(f"y_stored{i}") for i in range(2)]
        y_gathered = [sem(f"y_gathered{b}") for b in range(B)]
        xa_ready = sem("xa_ready")
        xa_transposed = sem("xa_transposed")
        xa_t_ready = sem("xa_t_ready")
        rkv_done = sem("rkv_done")
        ex_k_ready = sem("ex_k_ready")
        rk_read = sem("rk_read")
        ex_ready = sem("ex_ready")
        kv_ready = sem("kv_ready")
        u_k_ready = sem("u_k_ready")
        u_kv_ready = sem("u_kv_ready")
        gkv_ready = sem("gkv_ready")
        num_ready = sem("num_ready")
        den_ready = sem("den_ready")
        inv_ready = sem("inv_ready")
        gate_ready = sem("gate_ready")
        att_done = sem("att_done")
        x2_ready = sem("x2_ready")
        out_stored = sem("out_stored")

        def xn_written(engine, f, b):
            if f == 0:
                engine.wait_ge(xn_ready, b + 1)
                engine.wait_ge(xn_act_ready, b + 1)
                engine.wait_ge(xn_pool_ready, b + 1)
            elif b < ACT_BATCHES:
                engine.wait_ge(xn_act_ready, B + b + 1)
            else:
                engine.wait_ge(xn_ready, B + b - ACT_BATCHES + 1)

        def tile_here(engine, f, j):
            sems = tile_gathered2 if f else tile_gathered
            engine.wait_ge(sems[j % len(sems)], 16 * (j // len(sems) + 1))

        block = ctx.enter_context(nc.Block())

        @block.sync
        def _(sp):
            for b in range(B):
                sp.dma_start(x[:, BT * b:BT * (b + 1), :], x_tiles[:, BT * b:BT * (b + 1), :]).then_inc(x_loaded[b], 16)
                if b == 3:
                    sp.dma_start(cent[:, :], centroids).then_inc(cent_loaded, 16)
                    sp.dma_start(scale_c, ffn_scale.rearrange("(p a) -> p a", a=1)).then_inc(cent_loaded, 16)
            for src, dst in ((nu_log, nu_c), (gamma_log, gam_c), (b_rkv[0:P], br_c), (b_rkv[P:2 * P], bk_c),
                             (b_rkv[2 * P:3 * P], bv_c)):
                sp.dma_start(dst, src.rearrange("(p a) -> p a", a=1)).then_inc(cols_loaded, 16)
            sp.dma_start(up_raw[:, :, :], up_w.rearrange("e d h -> d e h")).then_inc(up_loaded, 16)
            sp.dma_start(down_raw[:, :, :, :], down_w.rearrange("e (c p) d -> p e c d", p=P)).then_inc(down_loaded, 16)
            sp.dma_start(wrkv[:, :], w_rkv).then_inc(attw_loaded, 16)
            sp.dma_start(wo[:, :], w_o).then_inc(attw_loaded, 16)
            for t in range(BT):
                sp.dma_start(bo_row[:, t * D:(t + 1) * D], b_o.rearrange("(a d) -> a d", a=1)).then_inc(attw_loaded, 16)
            for f in range(FFNS):
                for b in range(B):
                    xn_written(sp, f, b)
                    here = slice(BT * b, BT * (b + 1))
                    sp.dma_start(xn_tiles[f][:, here, 0:D], xn[:, here, :]).then_inc(xn_stored, 16)
                    if f == 1:
                        sp.wait_ge(base2_ready, b + 1)
                        sp.dma_start(xn_tiles[f][:, here, D:2 * D], x[:, here, :]).then_inc(xn_stored, 16)
                if f == 0:
                    for g in range(OUT_GROUPS):
                        sp.wait_ge(y_ready, OUT_GROUP * (g + 1))
                        s = OUT_GROUP * (g % 2)
                        sp.dma_start(y_tiles[:, OUT_GROUP * g:OUT_GROUP * (g + 1), :],
                                     y_out[:, s:s + OUT_GROUP, :]).then_inc(y_stored[g % 2], 16)
            sp.wait_ge(out_stored, 16 * SLOT_TILES)

        @block.gpsimd
        def _(pool):
            step = Counter(pool, const_made)
            step.mark(pool.memset(ident[:, :], 0.0))
            step.mark(pool.memset(ones_b[:, :], 1.0))
            step.mark(pool.memset(ones_f[:, :], 1.0))
            step.mark(pool.memset(not_before[:, :], -1.0))
            made = step.mark(pool.memset(within[:, :, :], 1.0))
            step.after(made)
            step.mark(pool.affine_select(out=ident[:, :], in_=ident[:, :], compare_op=ALU.not_equal, fill=1.0,
                                         base=0, pattern=[[-1, P]], channel_multiplier=1))
            step.mark(pool.affine_select(out=not_before[:, :], in_=not_before[:, :], compare_op=ALU.is_ge, fill=0.0,
                                         base=0, pattern=[[-1, P]], channel_multiplier=1))
            step.mark(pool.memset(within[:, :, 0:1], 0.0))
            low = dict(allow_small_or_imprecise_dtypes=True)
            step.mark(pool.iota(iota_slot[:, :, :], [[1, P], [0, X_TILES]], base=0, channel_multiplier=0, **low))
            step.mark(pool.iota(iota_tile[:, :, :], [[1, SLOT_TILES], [0, TILES]], base=0, channel_multiplier=0, **low))
            step.mark(pool.iota(no_token[:, :], [[0, 1]], base=TOKENS + 1, channel_multiplier=1, **low))
            step.mark(pool.iota(iota_part[:, :], [[0, 1]], base=1, channel_multiplier=1, **low))
            step.mark(pool.iota(iota_tok_tile[:, :], [[P, TILES]], base=0, channel_multiplier=0, **low))
            step.mark(pool.iota(rank_code[:, :, :], [[-1, E], [0, TILES]], base=E, channel_multiplier=0, **low))
            for g in range(X_GROUPS):
                pool.wait_ge(rows_ready, g + 1)
                r = first_rows[g]
                for i in range(2, X_TILES, BT):
                    t = X_TILES * g + i
                    pool.tensor_scalar(xn[:, t, :], x[:, t, :], r["val"][:, 1, i:i + 1], r["bias"][:, 1, i:i + 1],
                                       ALU.mult, ALU.add).then_inc(xn_pool_ready, 1)
            pool.wait_ge(up_hi_ready, 1)
            pool.tensor_tensor(up_lo[:, :], up_raw[:, :, :].rearrange("p e h -> p (e h)"),
                               up_hi[:, :].bitcast(F32), ALU.subtract).then_inc(up_lo_ready, 1)

            def gather_x(f, j):
                bufs = (gathered2[:, j % GATHER2_BUFS, :] if f else gathered[:, j % GATHER_BUFS, :])
                sems = tile_gathered2 if f else tile_gathered
                pool.indirect_dma_start(bufs, None, xn_dram[f],
                                        bass.IndirectOffsetOnAxis(ap=src_tok[:, j:j + 1], axis=0)
                                        ).then_inc(sems[j % len(sems)], 16)

            def gather_y(t):
                if t % BT == 0:
                    pool.wait_ge(base_ready, t // BT + 1)
                pool.indirect_dma_start(x[:, t, :], None, y_dram,
                                        bass.IndirectOffsetOnAxis(ap=pos_i[:, t:t + 1], axis=0),
                                        compute_op=ALU.add).then_inc(y_gathered[t // BT], 16)

            def scatter_out(j):
                pool.wait_ge(y_ready, SLOT_TILES + j + 1)
                pool.indirect_dma_start(out_rows, bass.IndirectOffsetOnAxis(ap=out_tok[:, j:j + 1], axis=0),
                                        out_buf(j), None, bounds_check=TOKENS - 1,
                                        oob_is_err=False).then_inc(out_stored, 16)

            def base2(b):
                pool.wait_ge(rows_ready, X_GROUPS + b + DEPTH + 1)
                xn_written(pool, 1, b)
                for t in range(BT * b, BT * (b + 1)):
                    last = pool.tensor_scalar(x[:, t, :], x[:, t, :], base_s[:, t:t + 1], base_b[:, t:t + 1],
                                              ALU.mult, ALU.add)
                last.then_inc(base2_ready, 1)

            def denominator(b):
                pool.wait_ge(u_k_ready, b + 1)
                pool.wait_ge(ex_ready, b + 1)
                step.after(step.mark(pool.tensor_tensor(den[:, :], u_k[:, b % 2, :], gk[:, b % 2, :], ALU.add)))
                if b >= 2:
                    pool.wait_ge(inv_ready, b - 1)
                pool.tensor_tensor(den_r[:, b % 2, :], den[:, :], ex_r1[:, b % 2, :], ALU.mult).then_inc(den_ready, 1)

            def gated(b):
                if b < DVE_SUMS:
                    pool.wait_ge(num_ready, b + 1)
                else:
                    pool.wait_ge(gkv_ready, b - DVE_SUMS + 1)
                    pool.wait_ge(u_kv_ready, b + 1)
                    step.after(step.mark(pool.tensor_tensor(num[:, b % 2, :], num[:, b % 2, :], u_kv[:, b % 2, :], ALU.add)))
                pool.wait_ge(inv_ready, b + 1)
                if b >= 2:
                    pool.wait_ge(att_done, b - 1)
                pool.tensor_tensor(gate_t[:, b % 2, :], num[:, b % 2, :], inv[:, b % 2, :], ALU.mult).then_inc(gate_ready, 1)

            pool.wait_ge(route_ready, 1)
            pool.wait_ge(xn_stored, 16 * B)
            for j in range(SLOT_TILES):
                if j >= GATHER_BUFS:
                    pool.wait_ge(xt_transposed, j - GATHER_BUFS + 1)
                gather_x(0, j)
            for s in range(2):
                pool.wait_ge(y_stored[s], 16 * sum(1 for g in range(OUT_GROUPS) if g % 2 == s))
            for t in range(Y_AHEAD * BT):
                gather_y(t)
            for i in range(B + DEPTH + 2):
                if 2 <= i < B + 2:
                    denominator(i - 2)
                if i > DEPTH + 1:
                    base2(i - DEPTH - 2)
                if i + Y_AHEAD < B:
                    for t in range(BT * (i + Y_AHEAD), BT * (i + Y_AHEAD + 1)):
                        gather_y(t)
                if 2 <= i < B + 2:
                    gated(i - 2)

            pool.wait_ge(route_ready, 2)
            pool.wait_ge(xn_stored, 16 * B * 3)
            for j in range(SLOT_TILES + SCATTER_LAG):
                if j < SLOT_TILES:
                    if j >= GATHER2_BUFS:
                        pool.wait_ge(y_ready, SLOT_TILES + j - GATHER2_BUFS + 1)
                    gather_x(1, j)
                if j == SCATTER_LAG:
                    pool.wait_ge(out_tok_ready, 1)
                if j >= SCATTER_LAG:
                    scatter_out(j - SCATTER_LAG)

        @block.scalar
        def _(act):
            step = Counter(act, act_step)
            act.preload_act_table_set("natural_log_exp_and_others")
            def columns():
                act.wait_ge(cols_loaded, 16 * 5)
                a = step.mark(nc.scalar.activation(col_tmp[:, 0:1], nu_c, ACT.Exp))
                nc.scalar.activation(col_tmp[:, 1:2], nu_c, ACT.Exp, bias=gam_c).then_inc(act_setup, 1)
                step.after(a)
                nc.scalar.activation(lam[:, :], col_tmp[:, 0:1], ACT.Exp, scale=-1.0).then_inc(act_setup, 1)
                nc.scalar.mul(neg_br[:, :], br_c, -1.0).then_inc(act_setup, 1)

            def transposed_copy(f, b):
                n = B * f + b
                act.wait_ge(xn_transposed, n + 1)
                if n >= 2:
                    act.wait_ge(scored, n - 1)
                nc.scalar.copy(xn_t[:, n % 2, :], (tr[1] if f else tr[n % 2])[:, :]).then_inc(xn_t_ready, 1)

            def base(t):
                b = t // BT
                xn_written(act, 0, b)
                last = nc.scalar.activation(x[:, t, :], x[:, t, :], ACT.Identity,
                                            bias=base_b[:, t:t + 1], scale=base_s[:, t:t + 1])
                if t % BT == BT - 1:
                    last.then_inc(base_ready, 1)

            def token_parts(f):
                act.wait_ge(in_tile_ready, f + 1)
                nc.scalar.activation(tok_id[:, SLOT_TILES:2 * SLOT_TILES, :], in_tile[:, :, :], ACT.Copy,
                                     scale=iota_part[:, :]).then_inc(tok_part_ready, 1)

            def seed(n, r):
                act.wait_ge(args_ready, n + 1)
                step.after(step.mark(nc.scalar.activation(r["log"][:, :, :], r["arg"][:, :, :], ACT.Ln)))
                nc.scalar.activation(r["val"][:, :, :], r["log"][:, :, :], ACT.Exp, scale=-0.5).then_inc(seed_ready, 1)

            def experts(f):
                def x_hi(j):
                    n = SLOT_TILES * f + j
                    act.wait_ge(xt_transposed, n + 1)
                    if n >= XT_BUFS:
                        act.wait_ge(up_done, n - XT_BUFS + 1)
                    nc.scalar.activation(xt_hi[:, n % XT_BUFS, :], tr[n % 2][:, 0:P], ACT.Copy,
                                         scale=scale_c).then_inc(xt_hi_ready, 1)

                def gate(j):
                    n = SLOT_TILES * f + j
                    act.wait_ge(up_done, n + 1)
                    if n >= 2:
                        act.wait_ge(hid_ready, n - 1)
                    nc.scalar.activation(silu[:, n % 2, :], up_ps[n % 2][:, HID:2 * HID], ACT.Silu).then_inc(silu_ready, 1)

                def h_copy(j):
                    n = SLOT_TILES * f + j
                    act.wait_ge(ht_transposed, n + 1)
                    if n >= HT_BUFS:
                        act.wait_ge(down_done, n - HT_BUFS + 1)
                    nc.scalar.copy(ht[:, n % HT_BUFS, :], ht_ps[n % 2][:, 0:2 * P]).then_inc(ht_ready, 1)

                x_hi(0)
                x_hi(1)
                for j in range(SLOT_TILES + 2):
                    if j < SLOT_TILES:
                        gate(j)
                    if j + 2 < SLOT_TILES:
                        x_hi(j + 2)
                    if j >= 2:
                        h_copy(j - 2)
                    if f == 0 and j < TILES:
                        base(j)

            seed(0, first_rows[0])
            for g in range(X_GROUPS):
                act.wait_ge(rows_ready, g + 1)
                r = first_rows[g]
                for i in range(1, X_TILES, 2):
                    t = X_TILES * g + i
                    last = nc.scalar.activation(xn[:, t, :], x[:, t, :], ACT.Identity,
                                                bias=r["bias"][:, 1, i:i + 1], scale=r["val"][:, 1, i:i + 1])
                    if t % BT == BT - 1:
                        last.then_inc(xn_act_ready, 1)
                if g == 0:
                    act.wait_ge(cent_made, 1)
                    nc.scalar.activation(cent_sq[:, :], cent_t[:, :], ACT.Square).then_inc(cent_squared, 1)
                transposed_copy(0, 2 * g)
                if g + 1 < X_GROUPS:
                    seed(g + 1, first_rows[g + 1])
                transposed_copy(0, 2 * g + 1)
            columns()
            act.wait_ge(up_loaded, 16)
            nc.scalar.copy(up_hi[:, :], up_raw[:, :, :].rearrange("p e h -> p (e h)")).then_inc(up_hi_ready, 1)
            act.wait_ge(down_loaded, 16)
            nc.scalar.mul(down_half[:, :], down_raw[:, :, :, :].rearrange("p e c d -> p (e c d)"), 0.5).then_inc(down_ready, 1)
            act.preload_act_table_set("silu_and_others")
            token_parts(0)
            experts(0)
            act.preload_act_table_set("natural_log_exp_and_others")

            def keys(b):
                act.wait_ge(rkv_done, 3 * b + 1)
                if b >= 2:
                    act.wait_ge(kv_ready, b - 1)
                    act.wait_ge(u_k_ready, b - 1)
                    act.wait_ge(den_ready, b - 1)
                nc.scalar.activation(ex_k[:, b % 2, :], k_ps[:, :], ACT.Exp, bias=bk_c).then_inc(ex_k_ready, 1)
                act.wait_ge(rkv_done, 3 * b + 3)
                if b >= 1:
                    act.wait_ge(ex_ready, b)
                nc.scalar.activation(ex_r[:, :], r_ps[:, :], ACT.Exp, bias=neg_br[:, :], scale=-1.0).then_inc(rk_read, 1)

            def keys_rest(b):
                act.wait_ge(ex_k_ready, b + 1)
                nc.scalar.activation(gk[:, b % 2, :], ex_k[:, b % 2, :], ACT.Identity, bias=den_eps[:, :], scale=gamma[:, :])
                act.wait_ge(rk_read, b + 1)
                nc.scalar.activation(ex_r1[:, b % 2, :], ex_r[:, :], ACT.Identity, bias=1.0).then_inc(ex_ready, 1)

            def normalise(i):
                if i < B:
                    r = rows[i % 2]
                    act.wait_ge(rows_ready, X_GROUPS + i + 1)
                    if i >= 2:
                        act.wait_ge(xa_transposed, i - 1)
                    for t in range(BT):
                        last = nc.scalar.activation(xa[:, i % 2, t, :], x[:, BT * i + t, :], ACT.Identity,
                                                    bias=r["bias"][:, 0, t:t + 1], scale=r["val"][:, 0, t:t + 1])
                    last.then_inc(xa_ready, 1)

            def gamma_kv(b):
                act.wait_ge(kv_ready, b + 1)
                if b >= 2:
                    act.wait_ge(gate_ready, b - 1)
                nc.scalar.activation(num[:, b % 2, :], kv[:, :], ACT.Copy, scale=gamma[:, :]).then_inc(gkv_ready, 1)

            def normalise_ffn(i):
                if DEPTH <= i < DEPTH + ACT_BATCHES:
                    r = rows[i % 2]
                    act.wait_ge(rows_ready, X_GROUPS + i + 1)
                    b = i - DEPTH
                    for t in range(BT):
                        last = nc.scalar.activation(xn[:, BT * b + t, :], x[:, BT * b + t, :], ACT.Identity,
                                                    bias=r["bias"][:, 2, t:t + 1], scale=r["val"][:, 2, t:t + 1])
                    last.then_inc(xn_act_ready, 1)

            for i in range(B + DEPTH):
                seed(X_GROUPS + i, rows[i % 2])
                if i > 0:
                    normalise_ffn(i - 1)
                normalise(i)
                if DVE_SUMS + 2 <= i < B + 2:
                    gamma_kv(i - 2)
                if 1 <= i <= B:
                    keys(i - 1)
                if i < B:
                    act.wait_ge(xa_transposed, i + 1)
                    if i >= 2:
                        act.wait_ge(rkv_done, 3 * (i - 1))
                    nc.scalar.copy(xa_t[:, i % 2, :], tr[0][:, :]).then_inc(xa_t_ready, 1)
                if 1 <= i <= B:
                    keys_rest(i - 1)
                if i > DEPTH:
                    transposed_copy(1, i - DEPTH - 1)
            transposed_copy(1, B - 1)
            act.preload_act_table_set("silu_and_others")
            token_parts(1)
            experts(1)

        @block.vector
        def _(dve):
            step = Counter(dve, dve_step)
            v = nc.vector

            def row_moments(r, k, i, t):
                return v.bn_stats(r["stats"][:, k, i, :], x[:, t, :])

            def rows_1(r, after=None):
                s = r["stats"]
                if after is not None:
                    step.after(after)
                step.mark(v.tensor_tensor(r["mean"][:, :, :], s[:, :, :, 1], s[:, :, :, 4], ALU.add))
                step.mark(v.tensor_tensor(r["diff"][:, :, :], s[:, :, :, 1], s[:, :, :, 4], ALU.subtract))
                return step.mark(v.tensor_tensor(r["var"][:, :, :], s[:, :, :, 2], s[:, :, :, 5], ALU.add))

            def rows_2(r, after):
                step.after(after)
                step.mark(v.tensor_scalar(r["mean"][:, :, :], r["mean"][:, :, :], 0.5, None, ALU.mult))
                return step.mark(v.scalar_tensor_tensor(r["diff"][:, :, :], r["diff"][:, :, :], 0.25, r["diff"][:, :, :],
                                                        ALU.mult, ALU.mult))

            def rows_3(r, after):
                step.after(after)
                return step.mark(v.scalar_tensor_tensor(r["var"][:, :, :], r["var"][:, :, :], 1.0 / D, r["diff"][:, :, :],
                                                        ALU.mult, ALU.add))

            def rows_4(r, after):
                step.after(after)
                return step.mark(v.tensor_scalar(r["arg"][:, 0:r["kinds"], :], r["var"][:, :, :], LN_EPS, None, ALU.add))

            def rows_5(r, after):
                k = r["kinds"]
                step.after(after)
                v.scalar_tensor_tensor(r["arg"][:, k, :], r["arg"][:, k - 1, :], RMS_EPS, r["var"][:, k - 1, :],
                                       ALU.mult, ALU.add).then_inc(args_ready, 1)

            def rows_6(n, r):
                dve.wait_ge(seed_ready, n + 1)
                return step.mark(v.tensor_tensor(r["tmp"][:, :, :], r["val"][:, :, :], r["val"][:, :, :], ALU.mult))

            def rows_7(r, after):
                step.after(after)
                return step.mark(v.scalar_tensor_tensor(r["tmp"][:, :, :], r["tmp"][:, :, :], -0.5, r["arg"][:, :, :],
                                                        ALU.mult, ALU.mult))

            def rows_8(r, after):
                step.after(after)
                return step.mark(v.scalar_tensor_tensor(r["val"][:, :, :], r["tmp"][:, :, :], 1.5, r["val"][:, :, :],
                                                        ALU.add, ALU.mult))

            def rows_9(r, t0, after):
                k, n = r["kinds"], r["n"]
                step.after(after)
                if k > 1:
                    step.mark(v.scalar_tensor_tensor(r["bias"][:, 0, :], r["mean"][:, 0, :], -1.0, r["val"][:, 0, :],
                                                     ALU.mult, ALU.mult))
                if t0 is not None:
                    step.mark(v.tensor_scalar(base_s[:, t0:t0 + n], r["val"][:, k - 1, :], 0.5, 1.0, ALU.mult, ALU.add))
                    step.mark(v.scalar_tensor_tensor(base_b[:, t0:t0 + n], r["mean"][:, k - 1, :], -0.5,
                                                     r["val"][:, k - 1, :], ALU.mult, ALU.mult))
                v.scalar_tensor_tensor(r["bias"][:, k, :], r["mean"][:, k - 1, :], -1.0, r["val"][:, k, :],
                                       ALU.mult, ALU.mult).then_inc(rows_ready, 1)

            by_token = "p e t -> p t e"

            def choose(f, b0, b1):
                t0, n = BT * b0, BT * (b1 - b0)
                here = (slice(None), slice(None), slice(t0, t0 + n))
                near = best[:, t0:t0 + n]
                wide = near.unsqueeze(1).to_broadcast([P, E, n])
                dve.wait_ge(scored, B * f + b1)
                step.after(step.mark(v.tensor_tensor(
                    score[here].rearrange(by_token),
                    score_ps[f][b0][:, t0 * E:(t0 + n) * E].rearrange("p (t e) -> p t e", e=E),
                    cnorm[:, :].unsqueeze(1).to_broadcast([P, n, E]), ALU.subtract)))
                step.after(step.mark(v.tensor_reduce(near, score[here].rearrange(by_token), axis=AX.X, op=ALU.max)))
                step.after(step.mark(v.tensor_tensor(code[here], score[here], wide, ALU.is_ge)))
                step.after(step.mark(v.tensor_tensor(code[here], code[here], rank_code[here], ALU.mult)))
                step.after(step.mark(v.tensor_reduce(near, code[here].rearrange(by_token), axis=AX.X, op=ALU.max)))
                last = v.tensor_tensor(onehot[here], code[here], wide, ALU.is_equal)
                if b1 == B:
                    last.then_inc(onehot_ready, 1)

            def route(f):
                dve.wait_ge(ranks_ready, f + 1)
                total = rank_ps[:, TILES * E:2 * TILES * E]
                csum2 = csum[:, :, :].rearrange("p e t -> p (e t)")
                slot2 = slot[:, :, :].rearrange("p e t -> p (e t)")
                step.after(step.mark(v.tensor_tensor_scan(csum2, within[:, :, :].rearrange("p e t -> p (e t)"), total, 0.0,
                                                          ALU.mult, ALU.add)))
                counted = step.mark(v.tensor_scalar(tiles_f[:, :], csum[:, :, TILES - 1], (P - 1) / 2, 1.0 / P,
                                                    ALU.add, ALU.mult))
                step.mark(v.tensor_tensor(slot2, csum2, rank_ps[:, 0:TILES * E], ALU.add))
                step.after(counted)
                step.after(step.mark(v.tensor_scalar(tiles_f[:, :], tiles_f[:, :], ROUND, ROUND, ALU.add, ALU.subtract)))
                step.after(step.mark(v.tensor_tensor_scan(tile_end[:, :], ones_f[:, 0:E], tiles_f[:, :], 0.0,
                                                          ALU.mult, ALU.add)))
                step.after(step.mark(v.tensor_tensor(tile_start[:, :], tile_end[:, :], tiles_f[:, :], ALU.subtract)))
                step.after(step.mark(v.scalar_tensor_tensor(slot[:, :, :], tile_start[:, :].unsqueeze(2).to_broadcast([P, E, TILES]),
                                                            float(P), slot[:, :, :], ALU.mult, ALU.add)))
                step.after(step.mark(v.tensor_tensor(slot2, slot2, onehot[:, :, :].rearrange("p e t -> p (e t)"), ALU.mult)))
                step.after(step.mark(v.tensor_reduce(pos[:, :], slot[:, :, :].rearrange(by_token), axis=AX.X, op=ALU.add)))
                part = step.mark(v.tensor_scalar(hi_f[:, :], pos[:, :], -(P - 1) / 2, 1.0 / P, ALU.add, ALU.mult))
                step.mark(v.tensor_copy(pos_i[:, :], pos[:, :]))
                step.after(part)
                step.after(step.mark(v.tensor_scalar(hi[:, :], hi_f[:, :], ROUND, ROUND, ALU.add, ALU.subtract)))
                v.scalar_tensor_tensor(lo[:, :], hi[:, :], -float(P), pos[:, :], ALU.mult, ALU.add).then_inc(lo_ready, 1)
                all_tiles = [P, SLOT_TILES, TILES]
                v.tensor_tensor(in_tile[:, :, :], iota_tile[:, :, :], hi[:, :].unsqueeze(1).to_broadcast(all_tiles),
                                ALU.is_equal).then_inc(in_tile_ready, 1)
                dve.wait_ge(in_tile_ready, f + 1)
                step.mark(v.tensor_tensor(tok_id[:, 0:SLOT_TILES, :], in_tile[:, :, :],
                                          iota_tok_tile[:, :].unsqueeze(1).to_broadcast(all_tiles), ALU.mult))
                dve.wait_ge(lo_ready, f + 1)
                for g in range(X_GROUPS):
                    v.tensor_tensor(in_slot[:, g, :, :], iota_slot[:, :, :],
                                    lo[:, X_TILES * g:X_TILES * (g + 1)].unsqueeze(1).to_broadcast([P, P, X_TILES]),
                                    ALU.is_equal).then_inc(in_slot_ready, 1)
                counted = step.mark(v.tensor_tensor(
                    past[:, :, :], iota_tile[0:1, :, 0:E],
                    tile_end[0:1, :].unsqueeze(1).to_broadcast([1, SLOT_TILES, E]), ALU.is_ge))
                dve.wait_ge(src_summed, f + 1)
                step.after(step.mark(v.tensor_reduce(src_sum[:, :], tr[0][:, 0:2 * SLOT_TILES].rearrange("p (a s) -> p s a", a=2),
                                                     axis=AX.X, op=ALU.add)))
                v.tensor_scalar(src_tok[:, :], src_sum[:, :], -1.0, 0.0, ALU.add, ALU.max).then_inc(route_ready, 1)
                step.after(counted)
                step.after(step.mark(v.tensor_reduce(exp_f[:, :], past[:, :, :], axis=AX.X, op=ALU.add)))
                v.tensor_scalar(exp_i[:, :], exp_f[:, :], float(E - 1), None, ALU.min).then_inc(experts_ready, 1)
                if f == 1:
                    step.after(step.mark(v.tensor_scalar(empty[:, :], src_sum[:, :], 0.0, no_token[:, :], ALU.is_equal, ALU.mult)))
                    v.scalar_tensor_tensor(out_tok[:, :], src_sum[:, :], -1.0, empty[:, :], ALU.add, ALU.add
                                           ).then_inc(out_tok_ready, 1)

            def experts(f):
                def x_lo(j):
                    n = SLOT_TILES * f + j
                    dve.wait_ge(xt_hi_ready, n + 1)
                    v.scalar_tensor_tensor(xt_lo[:, n % XT_BUFS, :], tr[n % 2][:, 0:P], scale_c,
                                           xt_hi[:, n % XT_BUFS, :].bitcast(F32), ALU.mult, ALU.subtract
                                           ).then_inc(xt_lo_ready, 1)

                def hidden(j):
                    n = SLOT_TILES * f + j
                    dve.wait_ge(silu_ready, n + 1)
                    if n >= HID_BUFS:
                        dve.wait_ge(ht_transposed, n - HID_BUFS + 1)
                    v.tensor_tensor(hid[:, n % HID_BUFS, :], up_ps[n % 2][:, 0:HID], silu[:, n % 2, :], ALU.mult).then_inc(hid_ready, 1)

                def y_copy(j):
                    n = SLOT_TILES * f + j
                    dve.wait_ge(down_done, n + 1)
                    if f == 1:
                        tile_here(dve, 1, j)
                        v.tensor_tensor(out_buf(j), y_ps[n % 2][:, 0:D], gathered2[:, j % GATHER2_BUFS, D:2 * D],
                                        ALU.add).then_inc(y_ready, 1)
                        return
                    g = j // OUT_GROUP
                    if j % OUT_GROUP == 0 and g >= 2:
                        dve.wait_ge(y_stored[g % 2], 16 * (g // 2))
                    s = OUT_GROUP * (g % 2) + j % OUT_GROUP
                    v.tensor_copy(y_out[:, s, :], y_ps[n % 2][:, 0:D]).then_inc(y_ready, 1)

                x_lo(0)
                x_lo(1)
                for j in range(SLOT_TILES + DOWN_LAG):
                    if j < SLOT_TILES:
                        hidden(j)
                    if j + 2 < SLOT_TILES:
                        x_lo(j + 2)
                    if j >= DOWN_LAG:
                        y_copy(j - DOWN_LAG)

            def set_up():
                dve.wait_ge(pe_setup, 1)
                v.tensor_copy(cent_t[:, :], rank_ps[:, 0:E]).then_inc(cent_made, 1)
                dve.wait_ge(cent_made, 1)
                dve.wait_ge(cent_loaded, 16 * 2)
                v.tensor_scalar(cent_rhs[:, :], cent_t[:, :], scale_c, 2.0, ALU.mult, ALU.mult).then_inc(dve_setup, 1)

            def decay_row():
                dve.wait_ge(act_setup, 3)
                step.mark(v.tensor_scalar(gamma[:, :], col_tmp[:, 1:2], -1.0, None, ALU.add))
                step.mark(v.tensor_scalar(lam_row[:, 0:TILES * E], ones_f[:, :], lam[:, :], None, ALU.mult))
                step.mark(v.tensor_scalar(lam_row[:, TILES * E:L], ones_f[:, 0:L - TILES * E], lam[:, :], None, ALU.mult))

            def first_moments(g, i):
                t = X_TILES * g + i
                if t % BT == 0:
                    dve.wait_ge(x_loaded[t // BT], 16)
                return row_moments(first_rows[g], 0, i, t)

            def first_rest(g, after, between):
                r = first_rows[g]
                a = rows_1(r, after)
                between(2)
                a = rows_2(r, a)
                between(1)
                a = rows_3(r, a)
                between(1)
                a = rows_4(r, a)
                between(1)
                rows_5(r, a)
                between(3)
                a = rows_6(g, r)
                a = rows_7(r, a)
                a = rows_8(r, a)
                rows_9(r, X_TILES * g, a)
                dve.wait_ge(rows_ready, g + 1)
                for i in range(0, X_TILES, BT):
                    t = X_TILES * g + i
                    v.tensor_scalar(xn[:, t, :], x[:, t, :], r["val"][:, 1, i:i + 1], r["bias"][:, 1, i:i + 1],
                                    ALU.mult, ALU.add).then_inc(xn_ready, 1)

            for r in rows:
                last = v.memset(r["stats"][:, :, :, :], 1.0)
            step.mark(last)
            v.memset(den_eps[:, :], DEN_EPS).then_inc(dve_setup, 1)
            done = 0
            for i in range(X_TILES):
                done = step.mark(first_moments(0, i))
            for g in range(X_GROUPS):
                ahead = []

                def next_moments(n):
                    if g + 1 < X_GROUPS:
                        for _ in range(n):
                            ahead.append(step.mark(first_moments(g + 1, len(ahead))))

                first_rest(g, done, next_moments)
                if g == 0:
                    set_up()
                if ahead:
                    done = ahead[-1]
            dve.wait_ge(const_made, 14)
            dve.wait_ge(pe_setup, 2)
            step.after(step.mark(v.tensor_copy(cnorm[:, :], rank_ps[:, E:2 * E])))
            for b0, b1 in ((0, 2), (2, 4), (4, 6), (6, 7), (7, 8)):
                choose(0, b0, b1)
            route(0)
            experts(0)

            decay_row()
            dve.wait_ge(attw_loaded, 16 * (2 + BT))
            step.mark(v.tensor_copy(ones_r[:, :], ones_f[0:1, 0:P]))
            part = step.mark(v.tensor_copy(bo_hi[:, :], bo_row[:, :]))
            step.after(part)
            v.tensor_tensor(bo_lo[:, :], bo_row[:, :], bo_hi[:, :].bitcast(F32), ALU.subtract).then_inc(dve_setup, 1)

            xv = x[:, :, :].rearrange("p t d -> p (t d)")
            moments = Counter(dve, moments_ready)

            def attention_moments(b, tiles):
                dve.wait_ge(y_gathered[b], 16 * BT)
                for t in tiles:
                    moments.mark(row_moments(rows[b % 2], 0, t, BT * b + t))

            for i in range(B + DEPTH):
                r = rows[i % 2]
                s = i - 2 if 2 <= i < B + 2 else None
                o = i - 4 if 4 <= i < B + 4 else None
                if i == 0:
                    attention_moments(0, range(BT))

                def next_moment(t):
                    if FILL <= i < B - 1:
                        attention_moments(i + 1, [t])

                if s is not None:
                    k = ex_k[:, s % 2, :]
                    dve.wait_ge(ex_k_ready, s + 1)
                    if s >= 2:
                        dve.wait_ge(den_ready, s - 1)
                    v.tensor_tensor_scan(u_k[:, s % 2, :], lam_row[:, :], k, 0.0, ALU.mult, ALU.add).then_inc(u_k_ready, 1)
                moments.after(moments.n)
                a = rows_1(r)
                if s is not None:
                    dve.wait_ge(rkv_done, 3 * s + 2)
                    if s > DVE_SUMS:
                        dve.wait_ge(gkv_ready, s - DVE_SUMS)
                    v.scalar_tensor_tensor(kv[:, :], v_ps[s % 2][:, :], bv_c, k, ALU.add, ALU.mult).then_inc(kv_ready, 1)
                a = rows_2(r, a)
                if s is not None:
                    dve.wait_ge(kv_ready, s + 1)
                    if s >= 2:
                        dve.wait_ge(gate_ready, s - 1)
                    v.tensor_tensor_scan(u_kv[:, s % 2, :], lam_row[:, :], kv[:, :], 0.0, ALU.mult, ALU.add).then_inc(u_kv_ready, 1)
                a = rows_3(r, a)
                next_moment(0)
                a = rows_4(r, a)
                next_moment(1)
                if s is not None and s < DVE_SUMS:
                    dve.wait_ge(u_kv_ready, s + 1)
                    if s >= 2:
                        dve.wait_ge(gate_ready, s - 1)
                    v.scalar_tensor_tensor(num[:, s % 2, :], kv[:, :], gamma[:, :], u_kv[:, s % 2, :],
                                           ALU.mult, ALU.add).then_inc(num_ready, 1)
                rows_5(r, a)
                if o is not None:
                    xb = xv[:, L * o:L * (o + 1)]
                    dve.wait_ge(att_done, o + 1)
                    dve.wait_ge(xa_ready, o + 1)
                    v.tensor_tensor(xb, xb, att_ps[:, :], ALU.add).then_inc(x2_ready, 1)
                a = rows_6(X_GROUPS + i, r)
                if o is not None:
                    nxt = rows[(i + 1) % 2]
                    dve.wait_ge(x2_ready, o + 1)
                    for t in range(BT):
                        moments.mark(row_moments(nxt, 1, t, BT * o + t))
                a = rows_7(r, a)
                next_moment(2)
                a = rows_8(r, a)
                next_moment(3)
                rows_9(r, BT * (i - DEPTH) if i >= DEPTH else None, a)
                if s is not None:
                    if s >= 2:
                        dve.wait_ge(gate_ready, s - 1)
                    dve.wait_ge(den_ready, s + 1)
                    v.reciprocal(inv[:, s % 2, :], den_r[:, s % 2, :]).then_inc(inv_ready, 1)
                if i < FILL:
                    attention_moments(i + 1, range(BT))
                if i >= DEPTH + ACT_BATCHES:
                    b = i - DEPTH
                    dve.wait_ge(rows_ready, X_GROUPS + i + 1)
                    for t in range(BT):
                        last = v.tensor_scalar(xn[:, BT * b + t, :], x[:, BT * b + t, :], r["val"][:, 2, t:t + 1],
                                               r["bias"][:, 2, t:t + 1], ALU.mult, ALU.add)
                    last.then_inc(xn_ready, 1)
                if i == B + 2:
                    choose(1, 0, 4)
            choose(1, 4, 7)
            choose(1, 7, 8)
            route(1)
            experts(1)

        @block.tensor
        def _(pe):
            mm = nc.tensor.matmul
            pe.wait_ge(const_made, 6)
            pe.wait_ge(cent_loaded, 16 * 2)
            nc.tensor.transpose(rank_ps[:, 0:E], cent[:, :], ident[0:E, 0:E]).then_inc(pe_setup, 1)

            def warm_up(bank, n):
                for _ in range(n):
                    mm(bank[:, :], ones_b[:, :], iota_slot[:, 0:L // X_TILES, :], start=True, stop=True)

            pe.wait_ge(const_made, 9)
            warm_up(ht_ps[1], 12)

            def xn_transpose(f, b):
                n = B * f + b
                xn_written(pe, f, b)
                if f:
                    pe.wait_ge(xn_t_ready, n)
                elif n >= 2:
                    pe.wait_ge(xn_t_ready, n - 1)
                for t in range(BT):
                    last = nc.tensor.transpose((tr[1] if f else tr[n % 2])[:, t * P:(t + 1) * P], xn[:, BT * b + t, :], ident[:, :])
                last.then_inc(xn_transposed, 1)

            def score_batch(f, b):
                n = B * f + b
                pe.wait_ge(xn_t_ready, n + 1)
                if f and score_ps[f][b] in (r_ps, k_ps):
                    pe.wait_ge(rk_read, B)
                for t in range(BT):
                    k = BT * b + t
                    last = mm(score_ps[f][b][:, k * E:(k + 1) * E], xn_t[:, n % 2, t * P:(t + 1) * P], cent_rhs[:, :],
                              start=True, stop=True)
                last.then_inc(scored, 1)

            def ranks(f):
                hot = onehot[:, :, :].rearrange("p e t -> p (e t)")
                pe.wait_ge(onehot_ready, f + 1)
                mm(rank_ps[:, 0:TILES * E], not_before[:, :], hot, start=True, stop=True)
                mm(rank_ps[:, TILES * E:2 * TILES * E], ones_b[:, :], hot, start=True, stop=True).then_inc(ranks_ready, 1)
                pe.wait_ge(tok_part_ready, f + 1)
                for t in range(TILES):
                    if t % X_TILES == 0:
                        pe.wait_ge(in_slot_ready, X_GROUPS * f + t // X_TILES + 1)
                    last = mm(tr[0][:, 0:2 * SLOT_TILES], in_slot[:, t // X_TILES, :, t % X_TILES], tok_id[:, :, t],
                              start=t == 0, stop=t == TILES - 1)
                last.then_inc(src_summed, 1)

            def load_expert(j):
                return nc.values_load(exp_i[0:1, j:j + 1], engines=(mybir.EngineType.PE,), min_val=0, max_val=E - 1,
                                      skip_runtime_bounds_check_because="a count of experts, cut at the last one")

            def experts(f):
                expert = {}

                def x_t(j):
                    n = SLOT_TILES * f + j
                    tile_here(pe, f, j)
                    if n >= 2:
                        pe.wait_ge(xt_lo_ready, n - 1)
                    nc.tensor.transpose(tr[n % 2][:, 0:P], slot_rows(f, j), ident[:, :]).then_inc(xt_transposed, 1)

                def up(j):
                    n = SLOT_TILES * f + j
                    pe.wait_ge(xt_lo_ready, n + 1)
                    if n >= 2:
                        pe.wait_ge(hid_ready, n - 1)
                    h, lo = (z[:, n % XT_BUFS, :] for z in (xt_hi, xt_lo))
                    at = bass.ds(expert[j] * (2 * HID), 2 * HID)
                    mm(up_ps[n % 2][:, :], h, up_hi[:, at], start=True, stop=False)
                    mm(up_ps[n % 2][:, :], h, up_lo[:, at], start=False, stop=False)
                    mm(up_ps[n % 2][:, :], lo, up_hi[:, at], start=False, stop=True).then_inc(up_done, 1)
                    if j + 2 < SLOT_TILES:
                        expert[j + 2] = load_expert(j + 2)

                def h_t(j):
                    n = SLOT_TILES * f + j
                    pe.wait_ge(hid_ready, n + 1)
                    if n >= 2:
                        pe.wait_ge(ht_ready, n - 1)
                    for c in range(2):
                        last = nc.tensor.transpose(ht_ps[n % 2][:, c * P:(c + 1) * P], hid[:, n % HID_BUFS, c * P:(c + 1) * P],
                                                   ident[:, :])
                    last.then_inc(ht_transposed, 1)

                def down(j):
                    n = SLOT_TILES * f + j
                    pe.wait_ge(ht_ready, n + 1)
                    if n >= 2:
                        pe.wait_ge(y_ready, n - 1)
                    for c in range(2):
                        at = bass.ds(expert[j] * (2 * D) + c * D, D)
                        last = mm(y_ps[n % 2][:, 0:D], ht[:, n % HT_BUFS, c * P:(c + 1) * P], down_half[:, at],
                                  start=c == 0, stop=c == 1)
                    last.then_inc(down_done, 1)

                pe.wait_ge(experts_ready, f + 1)
                warm_up(tr[0], 6)
                for j in range(2):
                    expert[j] = load_expert(j)
                x_t(0)
                x_t(1)
                warm_up(ht_ps[1], 3)
                pe.wait_ge(up_lo_ready, 1)
                pe.wait_ge(down_ready, 1)
                for j in range(SLOT_TILES + DOWN_LAG):
                    if j < SLOT_TILES:
                        up(j)
                    if j >= DOWN_LAG:
                        down(j - DOWN_LAG)
                    if j + 2 < SLOT_TILES:
                        x_t(j + 2)
                    if 0 <= j - 2 < SLOT_TILES:
                        h_t(j - 2)

            for b in range(B):
                xn_transpose(0, b)
                if b == 1:
                    pe.wait_ge(dve_setup, 2)
                    pe.wait_ge(cent_squared, 1)
                    mm(rank_ps[:, E:2 * E], ones_f[:, 0:P], cent_sq[:, :], start=True, stop=True).then_inc(pe_setup, 1)
                if b >= 1:
                    score_batch(0, b - 1)
                    warm_up(ht_ps[1], 2)
            score_batch(0, B - 1)
            ranks(0)
            experts(0)

            def xa_transpose(b):
                pe.wait_ge(xa_ready, b + 1)
                if b >= 1:
                    pe.wait_ge(xa_t_ready, b)
                for t in range(BT):
                    last = nc.tensor.transpose(tr[0][:, t * P:(t + 1) * P], xa[:, b % 2, t, :], ident[:, :])
                last.then_inc(xa_transposed, 1)

            def project(b):
                pe.wait_ge(xa_t_ready, b + 1)
                if b >= 1:
                    pe.wait_ge(rk_read, b)
                if b >= 2:
                    pe.wait_ge(kv_ready, b - 1)
                for i, bank in ((1, k_ps), (2, v_ps[b % 2]), (0, r_ps)):
                    mm(bank[:, :], wrkv[:, i * P:(i + 1) * P], xa_t[:, b % 2, :], start=True, stop=True).then_inc(rkv_done, 1)

            def att_out(b):
                pe.wait_ge(gate_ready, b + 1)
                if b >= 1:
                    pe.wait_ge(x2_ready, b)
                mm(att_ps[:, :], ones_r[:, :], bo_hi[:, :], start=True, stop=False)
                mm(att_ps[:, :], ones_r[:, :], bo_lo[:, :], start=False, stop=False)
                for t in range(BT):
                    last = mm(att_ps[:, t * D:(t + 1) * D], gate_t[:, b % 2, t * P:(t + 1) * P], wo[:, :], start=False, stop=t == BT - 1)
                last.then_inc(att_done, 1)

            pe.wait_ge(attw_loaded, 16 * (2 + BT))
            pe.wait_ge(dve_setup, 3)
            pe.wait_ge(y_gathered[0], 16 * BT)
            warm_up(tr[0], 12)
            for i in range(B + DEPTH):
                if i < B:
                    xa_transpose(i)
                if 3 <= i < B + 3:
                    att_out(i - 3)
                if i > DEPTH:
                    xn_transpose(1, i - DEPTH - 1)
                if i < B:
                    project(i)
                if i > DEPTH:
                    score_batch(1, i - DEPTH - 1)
            xn_transpose(1, B - 1)
            score_batch(1, B - 1)
            ranks(1)
            experts(1)


_INS = ['L0_attn_inputs', 'L0_attn_W_rkv', 'L0_attn_b_rkv', 'L0_attn_W_o', 'L0_attn_b_o', 'L0_attn_nu_log',
        'L0_attn_gamma_log', 'L0_ffn_scale', 'L0_ffn_centroids', 'L0_ffn_up_w', 'L0_ffn_down_w']


def kernel(**inputs):
    import concourse.bacc as _bacc
    from concourse.bass_utils import run_bass_kernel_spmd as _run

    nc = _bacc.Bacc("TRN2", target_bir_lowering=False, num_devices=1)
    arrays, args = {}, []
    for name in _INS:
        a = np.ascontiguousarray(inputs[name])
        arrays[f"in_{name}"] = a
        args.append(nc.dram_tensor(f"in_{name}", a.shape, mybir.dt.from_np(a.dtype), kind="ExternalInput").ap())
    out = nc.dram_tensor("out", (B, L, D), F32, kind="ExternalOutput").ap()
    macaron(nc, *args, out)
    r = _run(nc, [arrays], core_ids=[0])
    return r.results[0]["out"]
```
